# Optimizing a Trainium2 kernel written in Bass

```python
import numpy as np
import jax
import jax.numpy as jnp

def _softmax(x, axis=-1):
    return jax.nn.softmax(x, axis=axis)

def _gelu(x):
    return jax.nn.gelu(x, approximate=True)

def _silu(x):
    return jax.nn.silu(x)

def _sigmoid(x):
    return jax.nn.sigmoid(x)

def _layernorm(x, axis=-1, eps=1e-05):
    m = jnp.mean(x, axis=axis, keepdims=True)
    v = jnp.var(x, axis=axis, keepdims=True)
    return (x - m) / jnp.sqrt(v + eps)

def _scatter_add(tgt, idx, src, axis=0):
    return tgt.at[idx].add(src)

def _segment_sum(src, seg, n):
    return jax.ops.segment_sum(src, seg, n)
kernel_name = 'mk_decoder_preln_d2_seqx_r4_7da46f'

def setup_inputs(seed: int=0):
    np.random.seed(seed)
    _w = jnp.asarray

    def _rec_inputs():
        import jax
        import jax.numpy as jnp
        _rk = jax.random.key(seed)
        x = -0.0002928 + 1 * jax.random.normal(jax.random.fold_in(_rk, 1), (2, 1024, 256), jnp.float32)
        _lenS = 1024 - jax.random.randint(jax.random.fold_in(_rk, 7), (2,), 0, max(1, 1024 // 4) + 1, jnp.int32)
        _lenS2 = 154 - jax.random.randint(jax.random.fold_in(_rk, 8), (2,), 0, max(1, 154 // 4) + 1, jnp.int32)
        _ctx_1024P = jax.random.normal(jax.random.fold_in(_rk, 11), (2, 16, 256), jnp.float32)
        _ctx_1024c = jax.random.dirichlet(jax.random.fold_in(_rk, 511), 0.3 * jnp.ones((16,), jnp.float32), (2, 154))
        _ctx_1024t = jnp.einsum('bsk,bkd->bsd', _ctx_1024c, _ctx_1024P)
        _ctx_1024t = _ctx_1024t * jax.lax.rsqrt(jnp.mean(jnp.square(_ctx_1024t)) + 1e-12) * 0.953939
        ctx_1024 = -1.39393e-06 + 0.999914 * (_ctx_1024t + 0.3 * jax.random.normal(jax.random.fold_in(_rk, 611), (2, 154, 256), jnp.float32))
        _validS = jnp.arange(1024)[None, :] < _lenS[:, None]
        _validS2 = jnp.arange(154)[None, :] < _lenS2[:, None]
        _causal = jnp.tril(jnp.ones((1024, 1024), dtype=bool))
        mask_BxSxS2_bk1 = jnp.broadcast_to(_validS2[:, None, :], (2, 1024, 154))
        return (x, ctx_1024, mask_BxSxS2_bk1)
    x, ctx_1024, mask_BxSxS2_bk1 = _rec_inputs()

    def _L0_attn_setup():
        import jax, jax.numpy as jnp
        import numpy as np
        H = 4
        DK = 128
        DV = 64
        NH = 2
        HID = 256
        KSZ = 4
        EPS = 1e-05

        def short_conv(x, w):
            K = w.shape[1]
            T = x.shape[1]
            xp = jnp.pad(x, ((0, 0), (K - 1, 0), (0, 0)))
            y = sum((xp[:, i:i + T, :] * w[:, i] for i in range(K)))
            return jax.nn.silu(y)

        def l2norm(x, eps=1e-06):
            return x * jax.lax.rsqrt(jnp.sum(x * x, axis=-1, keepdims=True) + eps)
        key = jax.random.key(seed)
        ks = jax.random.split(key, 16)
        s = 0.02
        B, T = (2, 256)
        return {'hidden_states': jax.random.normal(ks[0], (B, T, HID), jnp.float32), 'Wq': jax.random.normal(ks[1], (HID, H * DK), jnp.float32) * s, 'Wk': jax.random.normal(ks[2], (HID, NH * H * DK), jnp.float32) * s, 'Wv': jax.random.normal(ks[3], (HID, NH * H * DV), jnp.float32) * s, 'Wb': jax.random.normal(ks[4], (HID, NH * H), jnp.float32) * s, 'Wa': jax.random.normal(ks[5], (HID, H), jnp.float32) * s, 'Wg': jax.random.normal(ks[6], (HID, H * DV), jnp.float32) * s, 'Wo': jax.random.normal(ks[7], (H * DV, HID), jnp.float32) * s, 'A_log': jnp.log(jax.random.uniform(ks[8], (H,), jnp.float32, 0.5, 8.0)), 'dt_bias': jax.random.normal(ks[9], (H,), jnp.float32) * 0.1, 'wq_conv': jax.random.normal(ks[10], (H * DK, KSZ), jnp.float32) * 0.2, 'wk_conv': jax.random.normal(ks[11], (NH * H * DK, KSZ), jnp.float32) * 0.2, 'wv_conv': jax.random.normal(ks[12], (NH * H * DV, KSZ), jnp.float32) * 0.2, 'o_norm_weight': jnp.ones((DV,), jnp.float32)}
    _L0_attn_all = _L0_attn_setup()
    _L0_attn_in = {k: v for k, v in _L0_attn_all.items() if k in ('Wq', 'Wk', 'Wv', 'Wb', 'Wa', 'Wg', 'Wo', 'A_log', 'dt_bias', 'wq_conv', 'wk_conv', 'wv_conv', 'o_norm_weight')}
    del _L0_attn_all

    def _L0_xattn_setup():
        import jax, jax.numpy as jnp
        import numpy as np
        EMBED_DIM = 256
        D_QKV = 64
        N_HEADS = 16
        SCALE = D_QKV ** 0.5
        key = jax.random.key(seed)
        ks = jax.random.split(key, 8)
        b, lq, lk, e = (2, 512, 512, EMBED_DIM)
        h, d = (N_HEADS, D_QKV)
        X = jax.random.normal(ks[0], (b, lq, e), dtype=jnp.float32)
        encoder_out = jax.random.normal(ks[1], (b, lk, e), dtype=jnp.float32)
        Wq = jax.random.normal(ks[2], (h * d, e), dtype=jnp.float32) * 0.02
        bq = jnp.zeros((h * d,), dtype=jnp.float32)
        Wkv = jax.random.normal(ks[3], (h * 2 * d, e), dtype=jnp.float32) * 0.02
        bkv = jnp.zeros((h * 2 * d,), dtype=jnp.float32)
        Wo = jax.random.normal(ks[4], (e, h * d), dtype=jnp.float32) * 0.02
        bo = jnp.zeros((e,), dtype=jnp.float32)
        return {'X': X, 'encoder_out': encoder_out, 'Wq': Wq, 'bq': bq, 'Wkv': Wkv, 'bkv': bkv, 'Wo': Wo, 'bo': bo}
    _L0_xattn_all = _L0_xattn_setup()
    _L0_xattn_in = {k: v for k, v in _L0_xattn_all.items() if k in ('Wq', 'bq', 'Wkv', 'bkv', 'Wo', 'bo')}
    del _L0_xattn_all

    def _L0_ffn_setup():
        import jax, jax.numpy as jnp
        import numpy as np
        B, L, H, E, FF, C = (4, 512, 256, 8, 1024, 2)
        key = jax.random.key(seed)
        ks = jax.random.split(key, 6)
        s = 0.02
        return {'x': jax.random.normal(ks[0], (B, L, H), dtype=jnp.float32), 'Wg': jax.random.normal(ks[1], (H, E), dtype=jnp.float32) * s, 'W1': jax.random.normal(ks[2], (E, H, FF), dtype=jnp.float32) * s, 'b1': jnp.zeros((E, FF), dtype=jnp.float32), 'W2': jax.random.normal(ks[3], (E, FF, H), dtype=jnp.float32) * s, 'b2': jnp.zeros((E, H), dtype=jnp.float32)}
    _L0_ffn_all = _L0_ffn_setup()
    _L0_ffn_in = {k: v for k, v in _L0_ffn_all.items() if k in ('Wg', 'W1', 'b1', 'W2', 'b2')}
    del _L0_ffn_all

    def _L1_attn_setup():
        import jax, jax.numpy as jnp
        import numpy as np
        N_HEADS = 16
        LOCAL_WINDOW = 128
        ROPE_BASE = 10000.0

        def _rotate_half(x):
            x1 = x[..., 0::2]
            x2 = x[..., 1::2]
            return jnp.stack((-x2, x1), axis=-1).reshape(x.shape)

        def _rope_cache(T, hd, dtype):
            half = hd // 2
            inv_freq = 1.0 / ROPE_BASE ** (jnp.arange(half, dtype=dtype) / half)
            t = jnp.arange(T, dtype=dtype)
            freqs = t[:, None] * inv_freq[None, :]
            cos = jnp.repeat(jnp.cos(freqs), 2, axis=-1)
            sin = jnp.repeat(jnp.sin(freqs), 2, axis=-1)
            return (cos, sin)
        key = jax.random.key(seed)
        k1, k2, k3, k4 = jax.random.split(key, 4)
        B, T, C = (2, 512, 256)
        x = jax.random.normal(k1, (B, T, C), dtype=jnp.float32)
        Wqkv = jax.random.normal(k2, (3 * C, C), dtype=jnp.float32) * 0.02
        Wproj = jax.random.normal(k3, (C, C), dtype=jnp.float32) * 0.02
        bproj = jax.random.normal(k4, (C,), dtype=jnp.float32) * 0.02
        return {'x': x, 'Wqkv': Wqkv, 'Wproj': Wproj, 'bproj': bproj}
    _L1_attn_all = _L1_attn_setup()
    _L1_attn_in = {k: v for k, v in _L1_attn_all.items() if k in ('Wqkv', 'Wproj', 'bproj')}
    del _L1_attn_all

    def _L1_xattn_setup():
        import jax, jax.numpy as jnp
        import numpy as np
        B, S, H, NH = (2, 512, 256, 16)
        DK = H // NH
        key = jax.random.key(seed)
        ks = jax.random.split(key, 12)
        scale = 0.02
        return {'Q': jax.random.normal(ks[0], (B, S, H), jnp.float32), 'K': jax.random.normal(ks[1], (B, S, H), jnp.float32), 'V': jax.random.normal(ks[2], (B, S, H), jnp.float32), 'attn_mask': jax.random.randint(ks[3], (B, S, S), 0, 2).astype(bool), 'Wq': jax.random.normal(ks[4], (H, H), jnp.float32) * scale, 'bq': jnp.zeros((H,), jnp.float32), 'Wk': jax.random.normal(ks[5], (H, H), jnp.float32) * scale, 'bk': jnp.zeros((H,), jnp.float32), 'Wv': jax.random.normal(ks[6], (H, H), jnp.float32) * scale, 'bv': jnp.zeros((H,), jnp.float32), 'Wo': jax.random.normal(ks[7], (H, H), jnp.float32) * scale, 'bo': jnp.zeros((H,), jnp.float32)}
    _L1_xattn_all = _L1_xattn_setup()
    _L1_xattn_in = {k: v for k, v in _L1_xattn_all.items() if k in ('Wq', 'bq', 'Wk', 'bk', 'Wv', 'bv', 'Wo', 'bo')}
    del _L1_xattn_all

    def _L1_ffn_setup():
        import jax, jax.numpy as jnp
        import numpy as np
        N_EXPERTS = 32
        TOP_K = 8
        N_GROUP = 4
        TOPK_GROUP = 2
        ROUTED_SCALING = 2.5

        def _gate(x, gate_w, gate_bias):
            T, E = (x.shape[0], gate_w.shape[0])
            logits = jnp.einsum('th,eh->te', x, gate_w)
            scores = jax.nn.sigmoid(logits)
            scores_choice = scores + gate_bias[None, :]
            grp = scores_choice.reshape(T, N_GROUP, E // N_GROUP)
            top2, _ = jax.lax.top_k(grp, 2)
            group_scores = top2.sum(-1)
            _, grp_idx = jax.lax.top_k(group_scores, TOPK_GROUP)
            group_mask = jax.nn.one_hot(grp_idx, N_GROUP, dtype=scores.dtype).sum(1)
            expert_mask = jnp.repeat(group_mask, E // N_GROUP, axis=1)
            masked = jnp.where(expert_mask > 0, scores_choice, 0.0)
            _, topk_idx = jax.lax.top_k(masked, TOP_K)
            topk_w = jnp.take_along_axis(scores, topk_idx, axis=1)
            topk_w = topk_w / (topk_w.sum(-1, keepdims=True) + 1e-20)
            topk_w = topk_w * ROUTED_SCALING
            return (topk_idx, topk_w)

        def _mlp(x, wg, wu, wd):
            return jnp.einsum('...i,hi->...h', jax.nn.silu(jnp.einsum('...h,ih->...i', x, wg)) * jnp.einsum('...h,ih->...i', x, wu), wd)
        key = jax.random.key(seed)
        ks = jax.random.split(key, 9)
        B, S, H, I = (2, 128, 256, 128)
        w = 0.02
        return {'hidden_states': jax.random.normal(ks[0], (B, S, H), jnp.float32), 'gate_w': jax.random.normal(ks[1], (N_EXPERTS, H), jnp.float32) * w, 'gate_bias': jax.random.normal(ks[2], (N_EXPERTS,), jnp.float32) * w, 'expert_gate': jax.random.normal(ks[3], (N_EXPERTS, I, H), jnp.float32) * w, 'expert_up': jax.random.normal(ks[4], (N_EXPERTS, I, H), jnp.float32) * w, 'expert_down': jax.random.normal(ks[5], (N_EXPERTS, H, I), jnp.float32) * w, 'shared_gate': jax.random.normal(ks[6], (2 * I, H), jnp.float32) * w, 'shared_up': jax.random.normal(ks[7], (2 * I, H), jnp.float32) * w, 'shared_down': jax.random.normal(ks[8], (H, 2 * I), jnp.float32) * w}
    _L1_ffn_all = _L1_ffn_setup()
    _L1_ffn_in = {k: v for k, v in _L1_ffn_all.items() if k in ('gate_w', 'gate_bias', 'expert_gate', 'expert_up', 'expert_down', 'shared_gate', 'shared_up', 'shared_down')}
    del _L1_ffn_all
    return {'x': x, 'ctx_1024': ctx_1024, 'mask_BxSxS2_bk1': mask_BxSxS2_bk1, 'L0_attn_Wq': _L0_attn_in['Wq'], 'L0_attn_Wk': _L0_attn_in['Wk'], 'L0_attn_Wv': _L0_attn_in['Wv'], 'L0_attn_Wb': _L0_attn_in['Wb'], 'L0_attn_Wa': _L0_attn_in['Wa'], 'L0_attn_Wg': _L0_attn_in['Wg'], 'L0_attn_Wo': _L0_attn_in['Wo'], 'L0_attn_A_log': _L0_attn_in['A_log'], 'L0_attn_dt_bias': _L0_attn_in['dt_bias'], 'L0_attn_wq_conv': _L0_attn_in['wq_conv'], 'L0_attn_wk_conv': _L0_attn_in['wk_conv'], 'L0_attn_wv_conv': _L0_attn_in['wv_conv'], 'L0_attn_o_norm_weight': _L0_attn_in['o_norm_weight'], 'L0_xattn_Wq': _L0_xattn_in['Wq'], 'L0_xattn_bq': _L0_xattn_in['bq'], 'L0_xattn_Wkv': _L0_xattn_in['Wkv'], 'L0_xattn_bkv': _L0_xattn_in['bkv'], 'L0_xattn_Wo': _L0_xattn_in['Wo'], 'L0_xattn_bo': _L0_xattn_in['bo'], 'L0_ffn_Wg': _L0_ffn_in['Wg'], 'L0_ffn_W1': _L0_ffn_in['W1'], 'L0_ffn_b1': _L0_ffn_in['b1'], 'L0_ffn_W2': _L0_ffn_in['W2'], 'L0_ffn_b2': _L0_ffn_in['b2'], 'L1_attn_Wqkv': _L1_attn_in['Wqkv'], 'L1_attn_Wproj': _L1_attn_in['Wproj'], 'L1_attn_bproj': _L1_attn_in['bproj'], 'L1_xattn_Wq': _L1_xattn_in['Wq'], 'L1_xattn_bq': _L1_xattn_in['bq'], 'L1_xattn_Wk': _L1_xattn_in['Wk'], 'L1_xattn_bk': _L1_xattn_in['bk'], 'L1_xattn_Wv': _L1_xattn_in['Wv'], 'L1_xattn_bv': _L1_xattn_in['bv'], 'L1_xattn_Wo': _L1_xattn_in['Wo'], 'L1_xattn_bo': _L1_xattn_in['bo'], 'L1_ffn_gate_w': _L1_ffn_in['gate_w'], 'L1_ffn_gate_bias': _L1_ffn_in['gate_bias'], 'L1_ffn_expert_gate': _L1_ffn_in['expert_gate'], 'L1_ffn_expert_up': _L1_ffn_in['expert_up'], 'L1_ffn_expert_down': _L1_ffn_in['expert_down'], 'L1_ffn_shared_gate': _L1_ffn_in['shared_gate'], 'L1_ffn_shared_up': _L1_ffn_in['shared_up'], 'L1_ffn_shared_down': _L1_ffn_in['shared_down']}

def reference(x, ctx_1024, mask_BxSxS2_bk1, L0_attn_Wq, L0_attn_Wk, L0_attn_Wv, L0_attn_Wb, L0_attn_Wa, L0_attn_Wg, L0_attn_Wo, L0_attn_A_log, L0_attn_dt_bias, L0_attn_wq_conv, L0_attn_wk_conv, L0_attn_wv_conv, L0_attn_o_norm_weight, L0_xattn_Wq, L0_xattn_bq, L0_xattn_Wkv, L0_xattn_bkv, L0_xattn_Wo, L0_xattn_bo, L0_ffn_Wg, L0_ffn_W1, L0_ffn_b1, L0_ffn_W2, L0_ffn_b2, L1_attn_Wqkv, L1_attn_Wproj, L1_attn_bproj, L1_xattn_Wq, L1_xattn_bq, L1_xattn_Wk, L1_xattn_bk, L1_xattn_Wv, L1_xattn_bv, L1_xattn_Wo, L1_xattn_bo, L1_ffn_gate_w, L1_ffn_gate_bias, L1_ffn_expert_gate, L1_ffn_expert_up, L1_ffn_expert_down, L1_ffn_shared_gate, L1_ffn_shared_up, L1_ffn_shared_down):
    import jax
    import jax.numpy as jnp

    def _L0_attn_ref(hidden_states, Wq, Wk, Wv, Wb, Wa, Wg, Wo, A_log, dt_bias, wq_conv, wk_conv, wv_conv, o_norm_weight):
        import jax, jax.numpy as jnp
        import numpy as np
        H = 4
        DK = 128
        DV = 64
        NH = 2
        HID = 256
        KSZ = 4
        EPS = 1e-05

        def short_conv(x, w):
            K = w.shape[1]
            T = x.shape[1]
            xp = jnp.pad(x, ((0, 0), (K - 1, 0), (0, 0)))
            y = sum((xp[:, i:i + T, :] * w[:, i] for i in range(K)))
            return jax.nn.silu(y)

        def l2norm(x, eps=1e-06):
            return x * jax.lax.rsqrt(jnp.sum(x * x, axis=-1, keepdims=True) + eps)
        B, T, _ = hidden_states.shape
        q = short_conv(hidden_states @ Wq, wq_conv).reshape(B, T, H, DK)
        k = short_conv(hidden_states @ Wk, wk_conv).reshape(B, T, NH, H, DK)
        v = short_conv(hidden_states @ Wv, wv_conv).reshape(B, T, NH, H, DV)
        q = l2norm(q)
        k = l2norm(k)
        beta = 2.0 * jax.nn.sigmoid(hidden_states @ Wb).reshape(B, T, NH, H)
        g = -jnp.exp(A_log) * jax.nn.softplus(hidden_states @ Wa + dt_bias)

        def step(S, x):
            q_t, k_t, v_t, b_t, g_t = x
            S = S * jnp.exp(g_t)[..., None, None]
            for i in range(NH):
                ki, vi, bi = (k_t[:, i], v_t[:, i], b_t[:, i])
                kv = jnp.einsum('bhk,bhkv->bhv', ki, S)
                S = S + bi[..., None, None] * jnp.einsum('bhk,bhv->bhkv', ki, vi - kv)
            o_t = jnp.einsum('bhk,bhkv->bhv', q_t, S)
            return (S, o_t)
        xs = (q.transpose(1, 0, 2, 3), k.transpose(1, 0, 2, 3, 4), v.transpose(1, 0, 2, 3, 4), beta.transpose(1, 0, 2, 3), g.transpose(1, 0, 2))
        S0 = jnp.zeros((B, H, DK, DV), hidden_states.dtype)
        _, o = jax.lax.scan(jax.checkpoint(step), S0, xs)
        o = o.transpose(1, 0, 2, 3)
        gate = (hidden_states @ Wg).reshape(B, T, H, DV)
        o = o * jax.lax.rsqrt(jnp.mean(o * o, axis=-1, keepdims=True) + EPS) * o_norm_weight
        o = o * jax.nn.silu(gate)
        return o.reshape(B, T, H * DV) @ Wo

    def _L0_xattn_ref(X, encoder_out, Wq, bq, Wkv, bkv, Wo, bo):
        import jax, jax.numpy as jnp
        import numpy as np
        EMBED_DIM = 256
        D_QKV = 64
        N_HEADS = 16
        SCALE = D_QKV ** 0.5
        b, lq, e = X.shape
        lk = encoder_out.shape[1]
        h, d = (N_HEADS, D_QKV)
        Q = (X @ Wq.T + bq).reshape(b, lq, h, d)
        KV = (encoder_out @ Wkv.T + bkv).reshape(b, lk, h, 2 * d)
        K, V = (KV[..., :d], KV[..., d:])
        scores = jnp.einsum('bqhd,bkhd->bhqk', Q, K) / SCALE
        weights = jax.nn.softmax(scores, axis=-1)
        attn = jnp.einsum('bhqk,bkhd->bqhd', weights, V).reshape(b, lq, h * d)
        out = attn @ Wo.T + bo
        return out

    def _L0_ffn_ref(x, Wg, W1, b1, W2, b2):
        import jax, jax.numpy as jnp
        import numpy as np
        B, L, H, E, FF, C = (4, 512, 256, 8, 1024, 2)
        b, l, h = x.shape
        e = Wg.shape[1]
        n = b * l
        k = min(max(int(n * C / e), 1), n)
        xt = x.reshape(n, h)
        S = jax.nn.sigmoid(xt @ Wg).T
        G, I = jax.lax.top_k(S, k)
        ex = xt[I]
        hid = jax.nn.gelu(jnp.einsum('ekh,ehf->ekf', ex, W1) + b1[:, None, :], approximate=False)
        out = (jnp.einsum('ekf,efh->ekh', hid, W2) + b2[:, None, :]) * G[..., None]
        new_x = jnp.zeros_like(xt).at[I.reshape(-1)].add(out.reshape(-1, h))
        return new_x.reshape(b, l, h)

    def _L1_attn_ref(x, Wqkv, Wproj, bproj):
        import jax, jax.numpy as jnp
        import numpy as np
        N_HEADS = 16
        LOCAL_WINDOW = 128
        ROPE_BASE = 10000.0

        def _rotate_half(x):
            x1 = x[..., 0::2]
            x2 = x[..., 1::2]
            return jnp.stack((-x2, x1), axis=-1).reshape(x.shape)

        def _rope_cache(T, hd, dtype):
            half = hd // 2
            inv_freq = 1.0 / ROPE_BASE ** (jnp.arange(half, dtype=dtype) / half)
            t = jnp.arange(T, dtype=dtype)
            freqs = t[:, None] * inv_freq[None, :]
            cos = jnp.repeat(jnp.cos(freqs), 2, axis=-1)
            sin = jnp.repeat(jnp.sin(freqs), 2, axis=-1)
            return (cos, sin)
        B, T, C = x.shape
        H = N_HEADS
        hd = C // H
        qkv = (x @ Wqkv.T).reshape(B, T, 3, H, hd).transpose(2, 0, 3, 1, 4)
        q, k, v = (qkv[0], qkv[1], qkv[2])
        cos, sin = _rope_cache(T, hd, x.dtype)
        cos = cos[None, None]
        sin = sin[None, None]
        q = q * cos + _rotate_half(q) * sin
        k = k * cos + _rotate_half(k) * sin
        scale = 1.0 / jnp.sqrt(jnp.asarray(hd, dtype=x.dtype))
        scores = jnp.einsum('bhqd,bhkd->bhqk', q, k) * scale
        i = jnp.arange(T)[:, None]
        j = jnp.arange(T)[None, :]
        allow = (j <= i) & (jnp.abs(i - j) <= LOCAL_WINDOW)
        scores = jnp.where(allow[None, None], scores, jnp.asarray(-jnp.inf, dtype=x.dtype))
        attn = jax.nn.softmax(scores, axis=-1)
        y = jnp.einsum('bhqk,bhkd->bhqd', attn, v)
        y = y.transpose(0, 2, 1, 3).reshape(B, T, C)
        return y @ Wproj.T + bproj

    def _L1_xattn_ref(Q, K, V, attn_mask, Wq, bq, Wk, bk, Wv, bv, Wo, bo):
        import jax, jax.numpy as jnp
        import numpy as np
        B, S, H, NH = (2, 512, 256, 16)
        DK = H // NH
        b = Q.shape[0]

        def proj(x, W, bias):
            return (x @ W.T + bias).reshape(b, -1, NH, DK).transpose(0, 2, 1, 3)
        q = proj(Q, Wq, bq)
        k = proj(K, Wk, bk)
        v = proj(V, Wv, bv)
        scores = jnp.einsum('bhqd,bhkd->bhqk', q, k) / jnp.sqrt(jnp.float32(DK))
        scores = jnp.where(attn_mask[:, None, :, :], jnp.float32(-1000000000.0), scores)
        attn = jax.nn.softmax(scores, axis=-1)
        ctx = jnp.einsum('bhqk,bhkd->bhqd', attn, v)
        ctx = ctx.transpose(0, 2, 1, 3).reshape(b, -1, NH * DK)
        return ctx @ Wo.T + bo

    def _L1_ffn_ref(hidden_states, gate_w, gate_bias, expert_gate, expert_up, expert_down, shared_gate, shared_up, shared_down):
        import jax, jax.numpy as jnp
        import numpy as np
        N_EXPERTS = 32
        TOP_K = 8
        N_GROUP = 4
        TOPK_GROUP = 2
        ROUTED_SCALING = 2.5

        def _gate(x, gate_w, gate_bias):
            T, E = (x.shape[0], gate_w.shape[0])
            logits = jnp.einsum('th,eh->te', x, gate_w)
            scores = jax.nn.sigmoid(logits)
            scores_choice = scores + gate_bias[None, :]
            grp = scores_choice.reshape(T, N_GROUP, E // N_GROUP)
            top2, _ = jax.lax.top_k(grp, 2)
            group_scores = top2.sum(-1)
            _, grp_idx = jax.lax.top_k(group_scores, TOPK_GROUP)
            group_mask = jax.nn.one_hot(grp_idx, N_GROUP, dtype=scores.dtype).sum(1)
            expert_mask = jnp.repeat(group_mask, E // N_GROUP, axis=1)
            masked = jnp.where(expert_mask > 0, scores_choice, 0.0)
            _, topk_idx = jax.lax.top_k(masked, TOP_K)
            topk_w = jnp.take_along_axis(scores, topk_idx, axis=1)
            topk_w = topk_w / (topk_w.sum(-1, keepdims=True) + 1e-20)
            topk_w = topk_w * ROUTED_SCALING
            return (topk_idx, topk_w)

        def _mlp(x, wg, wu, wd):
            return jnp.einsum('...i,hi->...h', jax.nn.silu(jnp.einsum('...h,ih->...i', x, wg)) * jnp.einsum('...h,ih->...i', x, wu), wd)
        orig_shape = hidden_states.shape
        H = orig_shape[-1]
        residuals = hidden_states
        x = hidden_states.reshape(-1, H)
        topk_idx, topk_w = _gate(x, gate_w, gate_bias)
        g = jnp.einsum('th,eih->eti', x, expert_gate)
        u = jnp.einsum('th,eih->eti', x, expert_up)
        outs = jnp.einsum('eti,ehi->eth', jax.nn.silu(g) * u, expert_down)
        outs_t = jnp.transpose(outs, (1, 0, 2))
        gathered = jnp.take_along_axis(outs_t, topk_idx[:, :, None], axis=1)
        final = (gathered * topk_w[:, :, None]).sum(1)
        shared = _mlp(residuals, shared_gate, shared_up, shared_down)
        return final.reshape(orig_shape) + shared
    x = x + _L0_attn_ref(_layernorm(x, axis=-1), L0_attn_Wq, L0_attn_Wk, L0_attn_Wv, L0_attn_Wb, L0_attn_Wa, L0_attn_Wg, L0_attn_Wo, L0_attn_A_log, L0_attn_dt_bias, L0_attn_wq_conv, L0_attn_wk_conv, L0_attn_wv_conv, L0_attn_o_norm_weight)
    x = x + _L0_xattn_ref(_layernorm(x, axis=-1), ctx_1024, L0_xattn_Wq, L0_xattn_bq, L0_xattn_Wkv, L0_xattn_bkv, L0_xattn_Wo, L0_xattn_bo)
    x = x + _L0_ffn_ref(_layernorm(x, axis=-1), L0_ffn_Wg, L0_ffn_W1, L0_ffn_b1, L0_ffn_W2, L0_ffn_b2)
    x = x + _L1_attn_ref(_layernorm(x, axis=-1), L1_attn_Wqkv, L1_attn_Wproj, L1_attn_bproj)
    x = x + _L1_xattn_ref(_layernorm(x, axis=-1), ctx_1024, ctx_1024, mask_BxSxS2_bk1, L1_xattn_Wq, L1_xattn_bq, L1_xattn_Wk, L1_xattn_bk, L1_xattn_Wv, L1_xattn_bv, L1_xattn_Wo, L1_xattn_bo)
    x = x + _L1_ffn_ref(_layernorm(x, axis=-1), L1_ffn_gate_w, L1_ffn_gate_bias, L1_ffn_expert_gate, L1_ffn_expert_up, L1_ffn_expert_down, L1_ffn_shared_gate, L1_ffn_shared_up, L1_ffn_shared_down)
    return x

_drawn_inputs = setup_inputs


def setup_inputs(seed=0):
    import zlib

    import numpy as np

    out = dict(_drawn_inputs(seed))
    spreads = {'L0_attn_o_norm_weight': (1.0, 0.6),
     'L0_xattn_bq': (0.0, 0.8),
     'L0_xattn_bkv': (0.0, 0.1),
     'L0_xattn_bo': (0.0, 0.1),
     'L0_ffn_b1': (0.0, 0.1),
     'L0_ffn_b2': (0.0, 0.1),
     'L1_xattn_bq': (0.0, 0.8),
     'L1_xattn_bk': (0.0, 0.8),
     'L1_xattn_bv': (0.0, 0.1),
     'L1_xattn_bo': (0.0, 0.1)}
    factors = {'L0_attn_Wb': 6.514,
     'L0_attn_Wa': 8.0,
     'L0_attn_A_log': 4.089,
     'L0_attn_dt_bias': 8.0,
     'L0_xattn_Wq': 7.789,
     'L1_attn_Wqkv': 3.028,
     'L1_attn_Wproj': 2.985,
     'L1_attn_bproj': 3.16,
     'L1_xattn_Wq': 8.0,
     'L1_xattn_Wk': 8.0,
     'L1_ffn_gate_w': 6.358,
     'L1_ffn_gate_bias': 8.0,
     'L1_ffn_expert_gate': 5.546,
     'L1_ffn_expert_up': 5.474,
     'L1_ffn_expert_down': 5.479,
     'L1_ffn_shared_gate': 3.477,
     'L1_ffn_shared_up': 3.44,
     'L1_ffn_shared_down': 3.42}
    for name, (base, spread) in spreads.items():
        noise = np.random.default_rng([zlib.crc32(name.encode()), seed]).standard_normal(out[name].shape)
        drawn = base * np.exp(spread * noise) if base else spread * noise
        out[name] = jnp.asarray(drawn.astype(out[name].dtype))
    for name, factor in factors.items():
        out[name] = (out[name] * factor).astype(out[name].dtype)
    return out
```

```python
from contextlib import ExitStack

import numpy as np

import concourse.bass as bass
from concourse import mybir

F32 = mybir.dt.float32
F32R = mybir.dt.float32r
BF16 = mybir.dt.bfloat16
I32 = mybir.dt.int32
U8 = mybir.dt.uint8
ALU = mybir.AluOpType
ACT = mybir.ActivationFunctionType
AX = mybir.AxisListType.X

P = 128
B, T, D = 2, 1024, 256
NT = B * T // P
TB = T // P
KD = D // P
S2 = 154
HALF = S2 // 2
EPS = 1e-5
NEG = -1e30

H, DK, DV, NH, KSZ = 4, 128, 64, 2, 4
CT = P // NH
NC = T // CT
NB = 8
BT_ = T // NB
CB = BT_ // CT
NCH = (H * DK + NH * H * DK + NH * H * DV) // P
LEVELS = [1, 2, 4, 8, 16, 32, 64]

XH, XD = 16, 64
NE0, FF, CAP = 8, 1024, 512
DIGIT = 3
AH, AD, WIN = 16, 16, 128
NE1, TOPK, NG, TOPG, FI, RSCALE = 32, 8, 4, 2, 128, 2.5
NSH = 2


def constant_arrays():
    p = np.arange(P)
    tok, par = p // NH, p % NH
    f = np.float32
    c = {}
    c["ident"] = np.eye(P, dtype=f)
    c["ones"] = np.ones((P, P), f)
    c["cum"] = ((par[:, None] == 0) & (tok[:, None] <= tok[None, :])).astype(f)
    c["tot"] = np.repeat((par == 0).astype(f)[:, None], P, 1)
    c["tri"] = (p[:, None] <= p[None, :]).astype(f)
    c["after"] = np.where(p[:, None] <= p[None, :], 0.0, NEG).astype(f)
    c["par"] = np.stack([par == 0, par == 1], 1).astype(f)
    inv = (f(1.0) / f(10000.0) ** (np.arange(AD // 2, dtype=f) / f(AD // 2))).astype(f)
    ang = (np.arange(T, dtype=f)[:, None] * inv[None, :]).astype(f)
    cos, sin = np.repeat(np.cos(ang), 2, 1), np.repeat(np.sin(ang), 2, 1)
    sin[:, 0::2] *= -1
    lay = lambda a: a.reshape(TB, P, AD).transpose(1, 0, 2).reshape(P, TB * AD)
    c["cos"], c["sin"] = lay(cos).astype(f), lay(sin).astype(f)
    c["earlier"] = np.repeat(np.tril(np.ones((NG, NG), f), -1).reshape(1, NG * NG), P, 0)
    patterns = [v << (30 - DIGIT * (b + 1)) for b in range(30 // DIGIT) for v in range(1, 2 ** DIGIT)]
    c["digits"] = np.repeat(np.array([patterns], np.int32).view(f), P, 0)
    wide = np.concatenate(list(c.values()), 1)
    at, n = {}, 0
    for k, a in c.items():
        at[k] = (n, a.shape[1])
        n += a.shape[1]
    masks = []
    for s in LEVELS:
        r, q = p[:, None], p[None, :]
        m = (r // (2 * s) == q // (2 * s)) & (r % (2 * s) >= s) & (q % (2 * s) < s)
        masks += [m, m.T]
    masks = np.concatenate(masks, 1)
    j = np.arange(2 * P)
    allow = np.where(j[None] < P, j[None] >= p[:, None], j[None] - P <= p[:, None])
    ids = np.stack([np.repeat(np.arange(NT)[None], P, 0), np.repeat(p[:, None], NT, 1)], 2)
    small = np.concatenate([np.eye(P), np.where(allow, 0.0, NEG), ids.reshape(P, -1)], 1)
    return wide, at, masks, small.astype(f)


class Step:

    def __init__(self, lane, emit, after):
        self.lane, self.emit, self.after = lane, emit, after
        self.sem, self.value, self.marked = lane.sem, None, False


class Lane:

    def __init__(self, sem, chained):
        self.sem, self.chained, self.steps, self.gate = sem, chained, [], ()
        self.previous = None

    def __call__(self, emit, *after):
        after, self.gate = after + (self.gate,), ()
        if self.chained:
            after += (self.previous,)
        step = self.previous = Step(self, emit, flat(after))
        self.steps.append(step)
        return step

    def last(self):
        return self.previous


class Transfer:

    def __init__(self, sem, value):
        self.sem, self.value = sem, value


class Channel:

    def __init__(self, sem):
        self.sem, self.count = sem, 0

    def start(self, lane, out, in_, *after, how=None, early=False):
        self.count += 16
        if not early:
            after, lane.gate = after + (lane.gate,), ()
        sem = self.sem
        if how is None:
            how = lambda e: e.dma_start(out, in_)
        step = Step(lane, lambda e: how(e).then_inc(sem, 16), flat(after))
        lane.steps.append(step)
        return Transfer(sem, self.count)


def flat(after):
    out = []
    for a in after:
        if a is None:
            continue
        out += flat(a) if isinstance(a, (tuple, list)) else [a]
    return out


class Ring:

    def __init__(self, aps):
        self.aps, self.free = aps, [(i, ()) for i in range(len(aps))]

    def take(self):
        assert self.free, "no buffer of the ring has been given back"
        i, steps = self.free.pop(0)
        return i, self.aps[i], steps

    def give(self, i, *steps):
        self.free.append((i, tuple(flat(steps))))


def need(*rings):
    while any(len(ring.free) < n for ring, n in rings):
        yield


def after(ready, generator):
    while not ready():
        yield
    yield from generator


def twice(generator):
    for _ in generator:
        next(generator, None)
        yield


def weave(generators, depth):
    waiting, running = list(generators), []
    while waiting or running:
        if waiting and len(running) < depth:
            running.append(waiting.pop(0))
        for g in list(running):
            try:
                next(g)
            except StopIteration:
                running.remove(g)


def program(nc, a, out, stages="ABCDEF"):
    _, at, _, _ = constant_arrays()
    with ExitStack() as ctx:
        def sem(name):
            return ctx.enter_context(nc.semaphore(name))

        def sb(name, shape, dt=F32, ctx=ctx):
            return ctx.enter_context(nc.sbuf_tensor(name, shape, dt))

        pe = Lane(sem("pe_done"), False)
        dve = Lane(sem("dve_done"), True)
        act = Lane(sem("act_done"), True)
        pool = Lane(sem("pool_done"), True)
        sp = Lane(sem("sp_done"), False)
        lanes = (pe, dve, act, pool, sp)
        banks = [ctx.enter_context(nc.psum_tensor(f"bank{i}", [P, 512], F32)) for i in range(8)]

        X = sb("X", [P, NT, D])
        wide = sb("wide", [P, a["wide"].shape[1]])
        masks = sb("masks", [P, len(LEVELS), 2, P], U8)
        small = sb("small", [P, a["small"].shape[1]])
        stats = sb("stats", [P, NT, 6])
        mv = sb("mv", [P, NT, 2])
        rs = sb("rs", [P, 4, NT])
        xn = sb("xn", [P, 2, 2, D])
        wa = sb("wa", [P, 8192])
        before_f = ctx.enter_context(ExitStack())
        wb = sb("wb", [P, 8192], ctx=before_f)
        XT = sb("XT", [P, KD, B * T], ctx=before_f)
        const = lambda k: wide[:, at[k][0]:at[k][0] + at[k][1]]
        ident, ones = const("ident"), const("ones")
        cos = const("cos").rearrange("p (t d) -> p t d", t=TB)
        sin = const("sin").rearrange("p (t d) -> p t d", t=TB)
        after_mask = const("after")

        ch = lambda name: Channel(sem(name))
        c_const, c_x = ch("const_in"), ch("x_in")
        const_in = [c_const.start(sp, wide[:, :], a["wide"]),
                    c_const.start(sp, small[:, :], a["small"]),
                    c_const.start(sp, masks[:].rearrange("p a b c -> p (a b c)"), a["masks"])][-1]
        x_in = c_x.start(sp, X[:, :, :], a["x"].rearrange("b (t p) d -> p (b t) d", p=P))

        def wait_all(lane_list=lanes):
            return [l.last() for l in lane_list]

        state = {"x": [x_in] * NT, "xt_free": (), "fence": (), "wa_free": ()}

        def mm(out_, lhsT, rhs, *after, start=True, stop=True, tp=None):
            return pe(lambda e: e.matmul(out_, lhsT, rhs, start=start, stop=stop, tile_position=tp,
                                         skip_group_check=True), *after)

        def tr(out_, in_, *after, idn=None):
            idn = ident if idn is None else idn
            k = in_.shape[0]
            return pe(lambda e: e.transpose(out_, in_, idn[0:k, 0:k]), *after)

        def tt(out_, x0, x1, op, *after, lane=dve):
            return lane(lambda e: e.tensor_tensor(out_, x0, x1, op), *after)

        def ts(out_, x0, s1, s2, op0, op1=ALU.bypass, *after, lane=dve):
            return lane(lambda e: e.tensor_scalar(out_, x0, s1, s2, op0, op1), *after)

        def stt(out_, x0, s, x1, op0, op1, *after):
            return dve(lambda e: e.scalar_tensor_tensor(out_, x0, s, x1, op0, op1), *after)

        def cp(lane, out_, in_, *after, scale=1.0):
            if lane is act:
                return act(lambda e: e.activation(out_, in_, ACT.Copy, scale=scale), *after)
            return lane(lambda e: e.tensor_copy(out_, in_), *after)

        def af(out_, in_, func, *after, bias=0.0, scale=1.0):
            return act(lambda e: e.activation(out_, in_, func, bias=bias, scale=scale), *after)

        def negmax(out_, in_, *after):
            return dve(lambda e: e.tensor_reduce(out_, in_, AX, ALU.max, negate=True), *after)

        def recip(out_, in_, *after):
            return dve(lambda e: e.reciprocal(out_, in_), *after)

        def pred(out_, mask, data, *after):
            return dve(lambda e: e.copy_predicated(out_, mask, data), *after)

        def bc(ap, n):
            return ap.unsqueeze(len(ap.shape)).broadcast_to(list(ap.shape) + [n])

        def rsqrt(v, r, t, *after):
            s = af(t, v, ACT.Ln, *after)
            s = af(r, t, ACT.Exp, s, scale=-0.5)
            s = tt(t, r, r, ALU.mult, s)
            s = tt(t, t, v, ALU.mult)
            s = ts(t, t, -0.5, 1.5, ALU.mult, ALU.add)
            return tt(r, r, t, ALU.mult)

        def layer_norm(ring, done, to_dram=None, parts=None):
            norm_free, stored = [(), ()], [None, None]
            for n in range(NT):
                dve(lambda e, n=n: e.bn_stats(stats[:, n, :], X[:, n, :]), state["x"][n])
                s = dve(lambda e, n=n: e.bn_aggr(mv[:, n, :], stats[:, n, :]))
            var, rstd, tmp = rs[:, 0, :], rs[:, 1, :], rs[:, 2, :]
            s = ts(var, mv[:, :, 1], EPS, None, ALU.add)
            rsqrt(var, rstd, tmp, s)
            yield
            for n2 in range(NT // 2):
                yield from need((ring, 1))
                buf = xn[:, n2 % 2]
                i, bank, free = ring.take()
                for m in range(2):
                    n = 2 * n2 + m
                    s = ts(buf[:, m, :], X[:, n, :], mv[:, n, 0:1], rstd[:, n:n + 1],
                           ALU.subtract, ALU.mult, norm_free[n2 % 2])
                    for k in range(KD):
                        t = tr(bank[:, (k * 2 + m) * P:(k * 2 + m + 1) * P],
                               buf[:, m, k * P:(k + 1) * P], s, free, const_in)
                at_ = slice(n2 * 2 * P, (n2 + 1) * 2 * P)
                src = bank[:, :].rearrange("p (k c) -> p k c", k=KD)
                if parts is None:
                    e = cp(act, XT[:, :, at_], src, t, state["xt_free"])
                else:
                    high, low = (part[:, :, at_] for part in parts)
                    e = cp(act, high, src, t)
                    e = tt(low, src, high.bitcast(F32), ALU.subtract, e)
                ring.give(i, e)
                norm_free[n2 % 2] = (t,)
                if to_dram is not None:
                    chans, dst = to_dram
                    stored[n2 % 2] = chans[n2 % 2].start(sp, dst[n2 * 2 * P:(n2 + 1) * 2 * P, :]
                                        .rearrange("(m p) d -> p m d", p=P), buf, s)
                    norm_free[n2 % 2] = (t, stored[n2 % 2])
                done += [e, e]
                yield
            return stored

        def until(done, n):
            while len(done) < n:
                yield

        def finish(generator):
            while True:
                try:
                    next(generator)
                except StopIteration as end:
                    return end.value

        c_w = {k: ch(f"weights_{k}_in") for k in ("A", "B", "B_keys", "B_values", "D", "E")}

        def load_weights(key, tensors, w, lo, *after):
            views, done = {}, None
            for name, part in tensors:
                k, n = a[name].shape[0] // part, a[name].shape[1]
                v = w[0:part, lo:lo + k * n].rearrange("p (k n) -> p k n", k=k)
                done = c_w[key].start(sp, v, a[name].rearrange("(k p) n -> p k n", p=part), *after, early=True)
                views[name], lo = v, lo + k * n
            return views, done, lo

        def rows(key, name, tile, *after, early=False):
            n = a[name].shape[0]
            src = a[name].rearrange("(o n) -> o n", o=1).broadcast_to([P, n])
            return c_w[key].start(sp, tile, src, *after, early=early)

        def load_layer_1(*after):
            state["weights_D"] = load_weights("D", [("d_wqkv", P), ("d_wo", P)], wb, 0, *after)
            state["weights_E"] = load_weights("E", [("e_wq", P), ("e_wk", P), ("e_wv", P), ("e_wo", P)], wb,
                                              2048, *after)

        def stage_a():
          with ExitStack() as sx:
            t_ = lambda name, shape, dt=F32: sb("a_" + name, shape, dt, ctx=sx)
            W, w_in, lo = load_weights("A", [("a_wqkv", P), ("a_wba", P), ("a_wg", P), ("a_wo", P)], wa, 0)
            convw = t_("convw", [P, NCH, KSZ])
            w_in = c_w["A"].start(sp, convw[:, :, :], a["a_conv"].rearrange("(c p) k -> p c k", p=P))
            alog, dtb, onw = t_("alog", [P, H]), t_("dtb", [P, H]), t_("onw", [P, DV])
            rows("A", "a_alog", alog[:, :]); rows("A", "a_dtb", dtb[:, :])
            w_in = rows("A", "a_onw", onw[:, :])

            ring = Ring([banks[i][:, :] for i in range(6)])
            xt = []
            finish(layer_norm(ring, xt))

            U4 = [P, B, NC, H]
            bt, g, G, gam = t_("bt", U4), t_("g", U4), t_("G", U4), t_("gam", U4)
            GCe, eKd = t_("GCe", U4), t_("eKd", U4)
            gamtok = t_("gamtok", [P, B, TB, H])
            z = t_("z", [P, B * NC, 12])
            za, zb = t_("za", [P, B * NC, H]), t_("zb", [P, B * NC, H])
            sq = t_("sq", [P, 2, 4 * P])
            dup = sq[:].rearrange("p a (k c) -> p (a k) c", c=P)[:, 0:4].rearrange("p (a k) c -> p k a c", a=2)
            decays = {}

            def decay_gates():
                i, bank, free = ring.take()
                dup_free = [(), ()]
                for u in range(B * NC):
                    for k in range(KD):
                        src = XT[:, k, u * CT:(u + 1) * CT]
                        s = dve(lambda e, src=src, k=k, u=u: e.tensor_copy(
                            dup[:, k, u % 2, :].rearrange("p (t i) -> p t i", i=NH), bc(src, NH)),
                            xt[u // 2], dup_free[u % 2])
                    for k in range(KD):
                        t = mm(bank[:, u * 12:u * 12 + 12], dup[:, k, u % 2, :], W["a_wba"][:, k, :],
                               s, free, w_in, start=k == 0, stop=k == KD - 1)
                    dup_free[u % 2] = (t,)
                    if u % 4 == 3:
                        yield
                decays["dup_read"] = t
                s = cp(dve, z[:, :, :], bank[:, 0:384].rearrange("p (u n) -> p u n", n=12), t)
                ring.give(i, s)
                beta = z[:, :, 0:2 * H]
                yield
                s = af(beta, beta, ACT.Exp, s, scale=-1.0)
                s = ts(beta, beta, 1.0, None, ALU.add, ALU.bypass, s)
                s = dve(lambda e: e.reciprocal(beta, beta))
                par = const("par")
                s = ts(za[:, :, :], beta[:, :, 0:H], par[:, 0:1], 2.0, ALU.mult, ALU.mult)
                s = ts(zb[:, :, :], beta[:, :, H:2 * H], par[:, 1:2], 2.0, ALU.mult, ALU.mult)
                fl = lambda x: x[:].rearrange("p b c h -> p (b c) h")
                s = tt(fl(bt), za[:, :, :], zb[:, :, :], ALU.add)
                yield
                zz = z[:, :, 2 * H:3 * H]
                s = tt(zz, zz, dtb[:, :].unsqueeze(1).broadcast_to([P, B * NC, H]), ALU.add)
                s = stt(za[:, :, :], zz, -1.0, zz, ALU.mult, ALU.max)
                s = af(za[:, :, :], za[:, :, :], ACT.Exp, s, scale=-1.0)
                s = af(za[:, :, :], za[:, :, :], ACT.Ln, s, bias=1.0)
                yield
                s1 = af(alog[:, :], alog[:, :], ACT.Exp, w_in)
                s = stt(za[:, :, :], zz, 0.0, za[:, :, :], ALU.max, ALU.add, s, s1)
                s = stt(fl(g), za[:, :, :], -1.0, alog[:, :].unsqueeze(1).broadcast_to([P, B * NC, H]),
                        ALU.mult, ALU.mult)
                yield
                i, bank, free = ring.take()
                gf = g[:].rearrange("p b c h -> p (b c h)")
                mm(bank[:, 0:P], const("cum"), gf, s, free, const_in)
                mm(bank[:, P:2 * P], const("tot"), gf)
                for half in range(2):
                    rhs = g[:].rearrange("p b (t e) h -> p b t e h", e=2)[:, :, :, half, :]
                    t = mm(bank[half * CT:(half + 1) * CT, 2 * P:2 * P + 64],
                           const("cum").rearrange("p (t i) -> p i t", i=NH)[:, 0, :], rhs)
                yield
                s = cp(dve, G[:].rearrange("p b c h -> p (b c h)"), bank[:, 0:P], t)
                s = tt(eKd[:].rearrange("p b c h -> p (b c h)"), bank[:, P:2 * P],
                       G[:].rearrange("p b c h -> p (b c h)"), ALU.subtract)
                e1 = af(GCe[:].rearrange("p b c h -> p (b c h)"), bank[:, P:2 * P], ACT.Exp, s)
                e1 = af(gamtok[:].rearrange("p b t h -> p (b t h)"), bank[:, 2 * P:2 * P + 64], ACT.Exp)
                ring.give(i, e1)
                e1 = af(eKd[:], eKd[:], ACT.Exp)
                decays["ready"] = af(gam[:], G[:], ACT.Exp)

            praw = t_("praw", [P, NCH, B, BT_ + KSZ - 1])
            acc = t_("acc", [P, 2, B, BT_])
            Qv = [t_(f"Qv{i}", [P, H, B, BT_]) for i in range(2)]
            Kv = [t_(f"Kv{i}", [P, H, B, BT_, NH]) for i in range(2)]
            Vv = [t_(f"Vv{i}", [P, NH, B, BT_, NH]) for i in range(2)]
            NK, NQ = B * CB * H, B * BT_ // P * H
            rk = [t_(f"rk{i}", [P, NK + NQ]) for i in range(2)]
            rv, rt = t_("rv", [P, NK + NQ]), t_("rt", [P, NK + NQ])
            coef = [t_(f"coef{i}", [P, 4, B, CB, H]) for i in range(2)]
            z0 = pool(lambda e: e.memset(praw[:, :, :, 0:KSZ - 1], 0.0))
            block_done = [None] * NB
            block_used = [()] * NB
            conv_read = [z0] * NCH

            def block(n):
                buf = n % 2
                lastv = None
                acc_free = [(), ()]
                for c in range(NCH):
                    i, bank, free = ring.take()
                    for bb in range(B):
                        for k in range(KD):
                            t = mm(bank[:, bb * BT_:(bb + 1) * BT_],
                                   W["a_wqkv"][:, k, c * P:(c + 1) * P],
                                   XT[:, k, bb * T + n * BT_:bb * T + (n + 1) * BT_],
                                   free, w_in, xt[bb * TB + (n + 1) * BT_ // P - 1],
                                   start=k == 0, stop=k == KD - 1)
                    if n > 0:
                        conv_read[c] = pool(lambda e, c=c: e.tensor_copy(
                            praw[:, c, :, 0:KSZ - 1], praw[:, c, :, BT_:BT_ + KSZ - 1]), conv_read[c])
                    s = cp(act, praw[:, c, :, KSZ - 1:], bank[:, 0:B * BT_].rearrange("p (b t) -> p b t", b=B),
                           t, conv_read[c])
                    ring.give(i, s)
                    A_ = acc[:, c % 2]
                    s = ts(A_, praw[:, c, :, 0:BT_], convw[:, c, 0:1], None, ALU.mult, ALU.bypass,
                           s, acc_free[c % 2])
                    for j in range(1, KSZ):
                        s = stt(A_, praw[:, c, :, j:j + BT_], convw[:, c, j:j + 1], A_, ALU.mult, ALU.add)
                    conv_read[c] = s
                    if c < H:
                        dst = Qv[buf][:, c]
                    elif c < H + NH * H:
                        dst = Kv[buf][:, (c - H) % H, :, :, (c - H) // H]
                    else:
                        v = c - H - NH * H
                        dst = Vv[buf][:, v % 2, :, :, v // 2]
                    s = af(dst, A_, ACT.Silu, s, block_used[n - 2] if n > 1 else ())
                    acc_free[c % 2] = (s,)
                    lastv = s
                    yield
                i, bank, free = ring.take()
                while "dup_read" not in decays:
                    yield
                sq_free = [(decays["dup_read"],)] * 2
                m = 0
                for h in range(2 * H):
                    src, first = (Kv[buf][:, h], 0) if h < H else (Qv[buf][:, h - H], NK)
                    src = src.rearrange("p b t i -> p (b t i)") if h < H else src.rearrange("p b t -> p (b t)")
                    width = src.shape[1]
                    s = tt(sq[:, m % 2, 0:width], src, src, ALU.mult, lastv, sq_free[m % 2])
                    for u in range(width // P):
                        col = first + u * H + h % H
                        t = mm(bank[:, col:col + 1], sq[:, m % 2, u * P:(u + 1) * P], ones[:, 0:1], s, free)
                    sq_free[m % 2] = (t,)
                    m += 1
                    if h % 2:
                        yield
                s = ts(rv[:, :], bank[:, 0:NK + NQ], 1e-6, None, ALU.add, ALU.bypass, t)
                ring.give(i, s)
                rsqrt(rv[:, :], rk[buf][:, :], rt[:, :], s, block_used[n - 2] if n > 1 else ())
                while "ready" not in decays:
                    yield
                r4 = rk[buf][:, 0:NK].rearrange("p (b c h) -> p b c h", b=B, c=CB)
                sl = slice(n * CB, (n + 1) * CB)
                C = coef[buf]
                s = tt(C[:, 0], r4, bt[:, :, sl, :], ALU.mult, decays["ready"])
                s = tt(C[:, 1], C[:, 0], gam[:, :, sl, :], ALU.mult)
                s = tt(C[:, 2], r4, eKd[:, :, sl, :], ALU.mult)
                s = ts(C[:, 3], r4, -1.0, None, ALU.mult)
                block_done[n] = (s, lastv)

            spare = [(wa, lo), (wb, NT * D)]
            Oacc = wb[:, 0:NT * D].rearrange("p (t d) -> p t d", t=NT)

            def four(name, n, k=2, w=None):
                bufs = []
                for i in range(k):
                    if w is None:
                        bufs.append(t_(f"{name}{i}", [P, H, n])[:, :, :])
                    else:
                        base, lo_ = spare[w]
                        assert lo_ + H * n <= 8192
                        bufs.append(base[:, lo_:lo_ + H * n].rearrange("p (h n) -> p h n", h=H))
                        spare[w] = (base, lo_ + H * n)
                return Ring(bufs)

            r_kb, r_kg, r_kd = four("kb", P, k=1, w=0), four("kg", P, w=1), four("kd", P, w=1)
            r_kbt, r_e, r_nt = four("kbt", P, k=1, w=0), four("e", P, k=1), four("nt", P, k=4)
            r_x, r_xt, r_y = four("x", P, k=4, w=1), four("xt", P, k=6), four("y", P, w=0)
            r_wt, r_bt, r_bv, r_u = four("wt", P), four("btm", CT, k=4), four("bv", DV, k=4), four("u", DV, w=0)
            St = t_("St", [P, B, H, DV])
            otmp = t_("otmp", [P, H, DV])
            ssq = t_("ssq", [P, 3, NT, H])
            s_ready = [pool(lambda e: e.memset(St[:, :, :, :], 0.0))] * B
            solved = {}
            fourbank = lambda bank: bank.rearrange("p (h n) -> p h n", h=H)

            prepared = {}

            def prepare(bb, c):
                n, cc, buf = c // CB, c % CB, (c // CB) % 2
                Kq, Qq, Vq, C = Kv[buf], Qv[buf], Vv[buf], coef[buf]
                ready = block_done[n]
                kc = [Kq[:, h, bb, cc * CT:(cc + 1) * CT, :].rearrange("p t i -> p (t i)") for h in range(H)]
                rk4 = rk[buf][:, 0:NK].rearrange("p (b c h) -> p b c h", b=B, c=CB)[:, bb, cc, :]
                yield from need((r_x, 1), (r_xt, 1), (r_nt, 1), (r_bt, 1), (r_bv, 1))
                ix, x, fx = r_x.take(); ixt, xtr, fxt = r_xt.take()
                idb = ident.unsqueeze(1).broadcast_to([P, H, P])
                p1 = cp(pool, x, idb, fx, const_in)
                p1 = cp(pool, xtr, idb, fxt)
                i, bank, free = ring.take()
                for h in range(H):
                    t = tr(fourbank(bank)[:, h, :], kc[h], ready, free)
                ikb, kb, fkb = r_kb.take()
                s = tt(kb, fourbank(bank), bc(C[:, 0, bb, cc, :], P), ALU.mult, t, fkb)
                ring.give(i, s)
                yield
                i2, bank2, free2 = ring.take()
                for h in range(H):
                    gc = g[:, bb, c, h:h + 1]
                    t2 = mm(fourbank(bank2)[:, h, :], gc.broadcast_to([P, P]), const("cum"), free2)
                ie, E, fe = r_e.take()
                for h in range(H):
                    s2 = stt(E[:, h, :], fourbank(bank2)[:, h, :], G[:, bb, c, h:h + 1], after_mask,
                             ALU.subtract, ALU.min, t2, fe)
                ring.give(i2, s2)
                se = af(E, E, ACT.Exp, s2)
                i, bank, free = ring.take()
                for h in range(H):
                    t = tr(fourbank(bank)[:, h, :], kb[:, h, :], s, free)
                r_kb.give(ikb, t)
                ikt, kbt, fkt = r_kbt.take()
                s = cp(act, kbt, fourbank(bank), t, fkt)
                ring.give(i, s)
                yield
                i, bank, free = ring.take()
                for h in range(H):
                    t = mm(fourbank(bank)[:, h, :], kc[h], kbt[:, h, :], s, free)
                r_kbt.give(ikt, t)
                int_, nt, fn = r_nt.take()
                for h in range(H):
                    s = stt(nt[:, h, :], fourbank(bank)[:, h, :], C[:, 3, bb, cc, h:h + 1], E[:, h, :],
                            ALU.mult, ALU.mult, t, se, fn)
                ring.give(i, s)
                yield
                mk = lambda l, w: masks[:, l, w, :].unsqueeze(1).broadcast_to([P, H, P])
                i, bank, free = ring.take()
                for h in range(H):
                    t = tr(fourbank(bank)[:, h, :], nt[:, h, :], s, free)
                s = pred(x, mk(0, 0), fourbank(bank), t, p1)
                ring.give(i, s)
                s = pred(xtr, mk(0, 1), nt)
                yield
                i, bank, free = ring.take()
                for h in range(H):
                    mm(bank[:, h * CT:(h + 1) * CT], kc[h], Qq[:, h, bb, cc * CT:(cc + 1) * CT], free)
                for v in range(2):
                    t = tr(bank[:, 2 * P + v * P:2 * P + (v + 1) * P],
                           Vq[:, v, bb, cc * CT:(cc + 1) * CT, :].rearrange("p t i -> p (t i)"))
                ib, btm, fb = r_bt.take(); iv, bv, fv = r_bv.take()
                for h in range(H):
                    sb_ = stt(btm[:, h, :], bank[:, h * CT:(h + 1) * CT], rk4[:, h:h + 1],
                              E[:, h, :].rearrange("p (t i) -> p i t", i=NH)[:, 1, :],
                              ALU.mult, ALU.mult, t, fb)
                r_e.give(ie, sb_)
                sv = tt(bv, bank[:, 2 * P:].rearrange("p (h d) -> p h d", h=H), bc(bt[:, bb, c, :], DV),
                        ALU.mult, fv)
                ring.give(i, sv)
                yield
                prepared[bb, c] = dict(x=(ix, x), xt=(ixt, xtr), nt=(int_, nt), bt=(ib, btm), bv=(iv, bv), kc=kc,
                                       C=C[:, :, bb, cc, :], ready=(s, sb_, sv))

            def solve(bb, c):
                while (bb, c) not in prepared:
                    yield
                q = prepared[bb, c]
                (ix, x), (ixt, xtr), (int_, nt) = (q[k] for k in ("x", "xt", "nt"))
                s = q["ready"]
                mk = lambda l, w: masks[:, l, w, :].unsqueeze(1).broadcast_to([P, H, P])
                for l in range(1, len(LEVELS)):
                    last = l == len(LEVELS) - 1
                    i, bank, free = ring.take()
                    for h in range(H):
                        t = mm(fourbank(bank)[:, h, :], nt[:, h, :], x[:, h, :], s, free)
                    iy, y, fy = r_y.take()
                    sy = cp(act, y, fourbank(bank), t, fy)
                    ring.give(i, sy)
                    yield
                    if not last:
                        i, bank, free = ring.take()
                        for h in range(H):
                            t = mm(fourbank(bank)[:, h, :], xtr[:, h, :], y[:, h, :], sy, free)
                    i2, bank2, free2 = ring.take()
                    for h in range(H):
                        t2 = mm(fourbank(bank2)[:, h, :], y[:, h, :], xtr[:, h, :], sy, free2)
                    r_y.give(iy, t2)
                    if l == len(LEVELS) - 3:
                        yield from need((r_kg, 1), (r_kd, 1))
                        ik, kbank, kfree = ring.take()
                        for h in range(H):
                            tk = tr(fourbank(kbank)[:, h, :], q["kc"][h], kfree)
                        ikg, kg, fkg = r_kg.take(); ikd, kd, fkd = r_kd.take()
                        sg = tt(kg, fourbank(kbank), bc(q["C"][:, 1], P), ALU.mult, tk, fkg)
                        sd = tt(kd, fourbank(kbank), bc(q["C"][:, 2], P), ALU.mult, fkd)
                        ring.give(ik, sd)
                    if not last:
                        s = pred(x, mk(l, 0), fourbank(bank), t)
                        ring.give(i, s)
                    s = pred(xtr, mk(l, 1), fourbank(bank2), t2)
                    ring.give(i2, s)
                    yield
                r_x.give(ix, t2); r_nt.give(int_, t2)
                i, bank, free = ring.take()
                for h in range(H):
                    t = mm(fourbank(bank)[:, h, :], kg[:, h, :], xtr[:, h, :], s, sg, free)
                r_kg.give(ikg, t)
                yield from need((r_wt, 1))
                iw, wt, fw = r_wt.take()
                sw = cp(act, wt, fourbank(bank), t, fw, scale=-1.0)
                ring.give(i, sw)
                solved[bb, c] = dict(q, wt=(iw, wt), kd=(ikd, kd), ready=(q["ready"], sw, s, sd))
                yield

            ubank, obank = banks[6][:, :], banks[7][:, :]
            bank_free = {"u": (), "o": ()}
            otmp_free = [(), ()]

            def advance(bb, c):
                while (bb, c) not in solved:
                    yield
                q = solved[bb, c]
                n, cc, buf = c // CB, c % CB, (c // CB) % 2
                xtr, wt, kd, btm, bv = (q[k][1] for k in ("xt", "wt", "kd", "bt", "bv"))
                Qc = [Qv[buf][:, h, bb, cc * CT:(cc + 1) * CT] for h in range(H)]
                row = slice((c % 2) * CT, (c % 2) * CT + CT)
                S = St[:, bb]
                for h in range(H):
                    mm(ubank[:, h * DV:(h + 1) * DV], xtr[:, h, :], bv[:, h, :], q["ready"], s_ready[bb],
                       bank_free["u"], start=True, stop=False)
                    t = mm(ubank[:, h * DV:(h + 1) * DV], wt[:, h, :], S[:, h, :], start=False, stop=True)
                r_xt.give(q["xt"][0], t); r_wt.give(q["wt"][0], t); r_bv.give(q["bv"][0], t)
                iu, u, fu = r_u.take()
                su = cp(act, u, ubank[:, 0:H * DV].rearrange("p (h d) -> p h d", h=H), t, fu)
                for h in range(H):
                    t1 = mm(obank[row, h * DV:(h + 1) * DV], Qc[h], S[:, h, :], bank_free["o"],
                            tp=(0, row.start))
                yield
                for h in range(H):
                    t = mm(ubank[:, (H + h) * DV:(H + h + 1) * DV], kd[:, h, :], u[:, h, :], su)
                for h in range(H):
                    to = mm(obank[row, (H + h) * DV:(H + h + 1) * DV], btm[:, h, :], u[:, h, :],
                            tp=(0, row.start))
                r_kd.give(q["kd"][0], t); r_bt.give(q["bt"][0], to); r_u.give(iu, to)
                s = tt(S, S, bc(GCe[:, bb, c, :], DV), ALU.mult, t1)
                s = tt(S, S, ubank[:, H * DV:].rearrange("p (h d) -> p h d", h=H), ALU.add, t)
                s_ready[bb] = s
                bank_free["u"] = (s, su)
                hb = lambda k: obank[row, k * H * DV:(k + 1) * H * DV].rearrange("p (h d) -> p h d", h=H)
                tile = bb * TB + c // 2
                ot = otmp[row]
                s = tt(ot, hb(0), bc(gamtok[row, bb, c // 2, :], DV), ALU.mult, to)
                s = tt(ot, ot, hb(1), ALU.add)
                bank_free["o"] = (s,)
                first = NK + (bb * (BT_ // P) + cc // 2) * H
                rq = rk[buf][row, first:first + H]
                s = tt(Oacc[row, tile, :].rearrange("p (h d) -> p h d", h=H), ot, bc(rq, DV), ALU.mult)
                if c % 2:
                    s = tt(xn[:, 0, 0, :], Oacc[:, tile, :], Oacc[:, tile, :], ALU.mult, s)
                    s = dve(lambda e: e.reduce_sum(
                        ssq[:, 0, tile, :], xn[:, 0, 0, :].rearrange("p (h d) -> p h d", h=H), AX))
                if bb == B - 1 and cc == CB - 1:
                    block_used[n] = (s, to)
                yield

            def scan():
                yield from chain(*[prepare(bb, 0) for bb in range(B)])
                for c in range(NC):
                    gens = [solve(bb, c) for bb in range(B)]
                    if c + 1 < NC:
                        gens += [after(lambda c=c: block_done[(c + 1) // CB] is not None,
                                       chain(*[prepare(bb, c + 1) for bb in range(B)]))]
                    if c:
                        gens += [chain(*[advance(bb, c - 1) for bb in range(B)])]
                    while gens:
                        for q in list(gens):
                            try:
                                next(q)
                            except StopIteration:
                                gens.remove(q)
                        yield
                for bb in range(B):
                    yield from advance(bb, NC - 1)

            def chain(*gens):
                for q in gens:
                    yield from q

            weave([decay_gates(), block(0)], 2)
            def rest():
                for n in range(1, NB):
                    while n > 1 and not block_used[n - 2]:
                        yield
                    yield from block(n)
            weave([scan(), twice(rest())], 2)

            OT = praw[:].rearrange("p a b c -> p (a b c)")[:, 0:KD * B * T].rearrange("p (k t) -> p k t", k=KD)
            scan_done = wait_all()
            v = ssq[:, 0].rearrange("p t h -> p (t h)")
            s = ts(v, v, 1.0 / DV, EPS, ALU.mult, ALU.add)
            s = rsqrt(v, ssq[:, 1].rearrange("p t h -> p (t h)"), ssq[:, 2].rearrange("p t h -> p (t h)"), s)
            rstd_ready = s
            gate_bufs = Ring([wb[:, NT * D + q * 2 * D:NT * D + (q + 1) * 2 * D].rearrange("p (m d) -> p m d", m=2)
                              for q in range(4)])

            def output(n2):
                i, bank, free = ring.take()
                for m in range(2):
                    for k in range(KD):
                        t = mm(bank[:, m * D:(m + 1) * D], XT[:, k, (2 * n2 + m) * P:(2 * n2 + m + 1) * P],
                               W["a_wg"][:, k, :], free, start=k == 0, stop=k == KD - 1)
                yield from need((gate_bufs, 1))
                ig, gt, fg = gate_bufs.take()
                s = af(gt, bank.rearrange("p (m d) -> p m d", m=2), ACT.Silu, t, rstd_ready, scan_done, fg)
                ring.give(i, s)
                g8 = gt.rearrange("p m (h d) -> p (m h) d", h=H)
                s = tt(g8, g8, onw[:, :].unsqueeze(1).broadcast_to([P, 2 * H, DV]), ALU.mult, s)
                s = tt(g8, g8, bc(ssq[:, 1, 2 * n2:2 * n2 + 2, :].rearrange("p t h -> p (t h)"), DV), ALU.mult)
                s = tt(gt, gt, Oacc[:, 2 * n2:2 * n2 + 2, :], ALU.mult)
                yield
                yield from need((ring, 1))
                i, bank, free = ring.take()
                for m in range(2):
                    for k in range(KD):
                        t = tr(bank[:, (k * 2 + m) * P:(k * 2 + m + 1) * P], gt[:, m, k * P:(k + 1) * P], s, free)
                gate_bufs.give(ig, t)
                s = cp(act, OT[:, :, n2 * 2 * P:(n2 + 1) * 2 * P], bank.rearrange("p (k c) -> p k c", k=KD), t,
                       conv_read)
                ring.give(i, s)
                yield
                yield from need((ring, 1))
                i, bank, free = ring.take()
                for m in range(2):
                    for k in range(KD):
                        t = mm(bank[:, m * D:(m + 1) * D], OT[:, k, (2 * n2 + m) * P:(2 * n2 + m + 1) * P],
                               W["a_wo"][:, k, :], s, free, start=k == 0, stop=k == KD - 1)
                xs = X[:, 2 * n2:2 * n2 + 2, :]
                s = tt(xs, xs, bank.rearrange("p (m d) -> p m d", m=2), ALU.add, t)
                ring.give(i, s)
                state["x"][2 * n2] = state["x"][2 * n2 + 1] = s

            weave([output(n2) for n2 in range(NT // 2)], 4)
            state["xt_free"] = (pe.last(),)
            state["fence"] = wait_all()

        def stage_b():
          with ExitStack() as sx:
            t_ = lambda name, shape, dt=F32: sb("b_" + name, shape, dt, ctx=sx)
            MT = XH * XD // P
            ctxT = t_("ctx", [P, KD, B * S2])
            bq, bk = t_("bq", [P, MT]), t_("bk", [P, MT])
            bv, bo = t_("bv", [P, XH * XD]), t_("bo", [P, D])
            W, k_in, lo = load_weights("B_keys", [("b_wk", P)], wb, 0, state["fence"])
            k_in = c_w["B_keys"].start(sp, ctxT[:, :, :], a["ctxT"].rearrange("(k p) n -> p k n", p=P))
            k_in = c_w["B_keys"].start(sp, bk[:, :], a["b_bk"])
            Wv, v_in, lo = load_weights("B_values", [("b_wv", P)], wb, lo, state["fence"])
            v_in = rows("B_values", "b_bv", bv[:, :])
            Wq, w_in, lo = load_weights("B", [("b_wq", P), ("b_wo", P)], wb, lo, state["fence"])
            w_in = c_w["B"].start(sp, bq[:, :], a["b_bq"]); w_in = rows("B", "b_bo", bo[:, :])
            W.update(Wv); W.update(Wq)

            ring = Ring([b_[:, :] for b_ in banks])
            KT = t_("KT", [P, MT, B * S2])
            V = t_("V", [HALF, B, 2, XH, XD + 1])
            kv_ready = [pool(lambda e: e.memset(V[:, :, :, :, XD:XD + 1], 1.0))]
            for m in range(MT):
                i, bank, free = ring.take()
                for k in range(KD):
                    t = mm(bank[:, 0:B * S2], W["b_wk"][:, k, m * P:(m + 1) * P], ctxT[:, k, :], free, k_in,
                           start=k == 0, stop=k == KD - 1)
                s = af(KT[:, m, :], bank[:, 0:B * S2], ACT.Identity, t, bias=bk[:, m:m + 1])
                ring.give(i, s)
            kv_ready.append(s)
            xt = []
            normed = layer_norm(ring, xt)
            next(normed)
            for bb in range(B):
                for hf in range(2):
                    for n in range(2):
                        i, bank, free = ring.take()
                        lo = bb * S2 + hf * HALF
                        for k in range(KD):
                            t = mm(bank[0:HALF, :], ctxT[:, k, lo:lo + HALF], W["b_wv"][:, k, n * 512:(n + 1) * 512],
                                   free, v_in, start=k == 0, stop=k == KD - 1)
                        s = tt(V[:, bb, hf, n * 8:(n + 1) * 8, 0:XD],
                               bank[0:HALF, :].rearrange("p (h d) -> p h d", d=XD),
                               bv[0:HALF, n * 512:(n + 1) * 512].rearrange("p (h d) -> p h d", d=XD), ALU.add, t)
                        ring.give(i, s)
            kv_ready.append(s)

            sc = XD ** -0.5
            s = ts(bq[:, :], bq[:, :], sc, None, ALU.mult, ALU.bypass, w_in)
            QB = 2 * P
            Q = Ring([t_(f"Q{i}", [P, MT, QB])[:, :, :] for i in range(2)])
            Pm = Ring([t_(f"P{i}", [P, 2, S2])[:] for i in range(6)])
            PTm = Ring([t_(f"PT{i}", [HALF, 2, 2, P])[:] for i in range(6)])
            mx, rec = t_("mx", [P, 6, 2]), t_("rec", [P, 4, 4])
            AO = Ring([t_(f"AO{i}", [P, XH, XD])[:, :, :] for i in range(2)])
            AOT = Ring([t_(f"AOT{i}", [P, MT, P])[:, :, :] for i in range(2)])
            qpair = {}

            def queries(n2):
                iq, q, fq = Q.take()
                yield from until(xt, 2 * n2 + 2)
                for m in range(MT):
                    i, bank, free = ring.take()
                    for k in range(KD):
                        t = mm(bank[:, 0:QB], W["b_wq"][:, k, m * P:(m + 1) * P],
                               XT[:, k, n2 * QB:(n2 + 1) * QB], free, xt[2 * n2], w_in,
                               start=k == 0, stop=k == KD - 1)
                    s1 = af(q[:, m, :], bank[:, 0:QB], ACT.Identity, t, s, fq, bias=bq[:, m:m + 1], scale=sc)
                    ring.give(i, s1)
                    yield
                qpair[n2] = (iq, q, s1)

            def unit(n, g4, par):
                while n // 2 not in qpair:
                    yield
                iq, q, qs = qpair[n // 2]
                q = q[:, :, (n % 2) * P:(n % 2 + 1) * P]
                bb = n // TB
                yield from need((Pm, 1), (ring, 1))
                ip, p_, fp = Pm.take()
                i, bank, free = ring.take()
                v = bank[:, 0:2 * S2].rearrange("p (h n) -> p h n", h=2)
                r = slice(par * XD, (par + 1) * XD)
                for j in range(2):
                    m = g4 * 2 + j
                    t = mm(v[:, j, :], q[r, m, :], KT[r, m, bb * S2:(bb + 1) * S2], free, qs, kv_ready,
                           tp=(par * XD, 0))
                mxs = mx[:, ip, :]
                s = negmax(mxs, v, t, fp)
                for j in range(2):
                    s = af(p_[:, j, :], v[:, j, :], ACT.Exp, s, fp, bias=mx[:, ip, j:j + 1])
                ring.give(i, s)
                yield
                yield
                yield from need((PTm, 1), (ring, 1))
                i, bank, free = ring.take()
                v = bank[0:HALF, :].rearrange("p (a b c) -> p a b c", a=2, b=2)
                for j in range(2):
                    for hf in range(2):
                        t = tr(v[:, j, hf, :], p_[:, j, hf * HALF:(hf + 1) * HALF], s, free)
                ipt, pt, fpt = PTm.take()
                s2 = cp(dve, pt, v, t, fpt)
                ring.give(i, s2)
                Pm.give(ip, t)
                yield
                yield
                if g4 not in groups[n]:
                    yield from need((ring, 1))
                    groups[n][g4] = [ring.take(), 0]
                i, bank, free = groups[n][g4][0]
                v = bank[:, 0:4 * (XD + 1)].rearrange("p (h n) -> p h n", h=4)
                for j in range(2):
                    for hf in range(2):
                        t = mm(v[:, 2 * j + par, :], pt[:, j, hf, :], V[:, bb, hf, g4 * 4 + 2 * j + par, :], s2, free,
                               start=hf == 0, stop=hf == 1)
                PTm.give(ipt, t)
                groups[n][g4][1] += 1
                if groups[n][g4][1] == 2:
                    if n not in aos:
                        yield from need((AO, 1))
                        aos[n] = AO.take()
                    _, ao, fao = aos[n]
                    rs_ = rec[:, g4, :]
                    recip(rs_, v[:, :, XD], t)
                    s = tt(ao[:, g4 * 4:(g4 + 1) * 4, :], v[:, :, 0:XD], bc(rs_, XD), ALU.mult, fao)
                    ring.give(i, s)
                    ao_done[n].append((s, t))

            def finish(n):
                while len(ao_done[n]) < XH // 4:
                    yield
                iq = qpair[n // 2][0]
                if n % 2:
                    Q.give(iq, ao_done[n][-1][1])
                iao, ao, _ = aos[n]
                yield from need((AOT, 1))
                iat, at_, fat = AOT.take()
                for hlf in range(2):
                    yield from need((ring, 1))
                    i, bank, free = ring.take()
                    for m in range(4):
                        mm_ = hlf * 4 + m
                        t = tr(bank[:, m * P:(m + 1) * P],
                               ao.rearrange("p h d -> p (h d)")[:, mm_ * P:(mm_ + 1) * P], ao_done[n][-1][0], free)
                    s2 = cp(act, at_[:, hlf * 4:(hlf + 1) * 4, :], bank.rearrange("p (m c) -> p m c", m=4), t, fat)
                    ring.give(i, s2)
                    yield
                AO.give(iao, t)
                yield
                yield from need((ring, 1))
                i, bank, free = ring.take()
                for m in range(MT):
                    t = mm(bank[:, 0:D], at_[:, m, :], W["b_wo"][:, m, :], s2, free, start=m == 0, stop=m == MT - 1)
                AOT.give(iat, t)
                s = tt(X[:, n, :], X[:, n, :], bo[:, :], ALU.add, w_in)
                s = tt(X[:, n, :], X[:, n, :], bank[:, 0:D], ALU.add, t)
                ring.give(i, s)
                state["x"][n] = s

            groups, aos, ao_done = [{} for _ in range(NT)], {}, [[] for _ in range(NT)]
            gens = [queries(0)]
            for n in range(NT):
                if n % 2 == 0 and n // 2 + 1 < NT // 2:
                    gens.append(after(lambda n=n: n < 2 or bool(ao_done[n - 1][3:]), queries(n // 2 + 1)))
                gens += [unit(n, g4, par) for g4 in range(XH // 4) for par in range(2)] + [finish(n)]
            weave([normed] + gens, 9)
            state["xt_free"] = (pe.last(),)
            state["fence"] = wait_all()
            load_layer_1(*state["fence"])

        def stage_d():
          with ExitStack() as sx:
            t_ = lambda name, shape, dt=F32: sb("d_" + name, shape, dt, ctx=sx)
            W, w_in, _ = state["weights_D"]
            bo = t_("bo", [P, D])
            w_in = rows("D", "d_bo", bo[:, :])
            ring = Ring([b_[:, :] for b_ in banks])
            xt = []
            normed = layer_norm(ring, xt)
            smallb = t_("smallb", [P, 3 * P], BF16)
            m_in = cp(dve, smallb[:, :], small[:, 0:3 * P], const_in)
            identb, window = smallb[:, 0:P], smallb[:, P:3 * P]
            qk = [t_(f"qk{i}", [P, 2, AH, 32]) for i in range(2)]
            z0 = [pool(lambda e, i=i: e.memset(qk[i][:, :, :, :], 0.0)) for i in range(2)]
            NQ4 = AH // 4
            QT = t_("QT", [P, NQ4, 3, P])
            KT = t_("KT", [P, NQ4, 3, P])
            V = t_("V", [P, 3, AH, 32])
            pool(lambda e: e.memset(V[:, :, :, AD:], 0.0))
            v1 = pool(lambda e: e.memset(V[:, :, :, AD:AD + 1], 1.0))
            OTm = Ring([t_(f"OT{i}", [P, 2, P])[:, :, :] for i in range(2)])
            raw, rot = t_("raw", [P, 2 * D]), t_("rot", [P, 2 * D])
            raw_free = ()
            Pm = Ring([t_(f"P{i}", [P, 2, 2 * P])[:] for i in range(8)])
            PTm = Ring([t_(f"PT{i}", [P, 2, 2 * P])[:] for i in range(8)])
            mx = t_("mx", [P, 8, 2])
            rec = t_("rec", [P, 8])
            AO = Ring([t_(f"AO{i}", [P, AH, AD])[:, :, :] for i in range(2)])
            AOT = Ring([t_(f"AOT{i}", [P, KD, P])[:, :, :] for i in range(2)])
            made = {}
            slot_free = [(), (), ()]
            qk_free = [(), ()]

            def project(n):
                nonlocal raw_free
                slot = n % 3
                yield from until(xt, n + 1)
                i, bank, free = ring.take()
                i2, bank2, free2 = ring.take()
                for k in range(KD):
                    mm(bank[:, :], XT[:, k, n * P:(n + 1) * P], W["d_wqkv"][:, k, 0:2 * D], free, xt[n], w_in,
                       start=k == 0, stop=k == KD - 1)
                for k in range(KD):
                    t = mm(bank2[:, 0:D], XT[:, k, n * P:(n + 1) * P], W["d_wqkv"][:, k, 2 * D:3 * D], free2,
                           start=k == 0, stop=k == KD - 1)
                s = cp(act, raw[:, :], bank, t, raw_free)
                ring.give(i, s)
                sv = cp(act, V[:, slot, :, 0:AD], bank2[:, 0:D].rearrange("p (h d) -> p h d", d=AD), t,
                        v1, slot_free[slot])
                ring.give(i2, sv)
                r3 = raw[:, :].rearrange("p (h d) -> p h d", d=AD)
                o3 = rot[:, :].rearrange("p (h d) -> p h d", d=AD)
                cb = cos[:, n % TB, :].unsqueeze(1).broadcast_to([P, 2 * AH, AD])
                sn = sin[:, n % TB, :].rearrange("p (d i) -> p d i", i=2)
                r4 = raw[:, :].rearrange("p (h d i) -> p h d i", h=2 * AH, i=2)
                o4 = rot[:, :].rearrange("p (h d i) -> p h d i", h=2 * AH, i=2)
                hb = [P, 2 * AH, AD // 2]
                s = tt(o4[:, :, :, 0], r4[:, :, :, 1], sn[:, :, 0].unsqueeze(1).broadcast_to(hb), ALU.mult, s)
                s = tt(o4[:, :, :, 1], r4[:, :, :, 0], sn[:, :, 1].unsqueeze(1).broadcast_to(hb), ALU.mult)
                s = tt(r3, r3, cb, ALU.mult)
                q_ = qk[n % 2]
                s = tt(q_[:, :, :, 0:AD].rearrange("p a h d -> p (a h) d"), r3, o3, ALU.add, qk_free[n % 2], z0)
                raw_free = (s,)
                yield
                for a_, dst in ((0, QT), (1, KT)):
                    i, bank, free = ring.take()
                    for m in range(NQ4):
                        t = tr(bank[:, m * P:(m + 1) * P],
                               q_[:, a_, m * 4:(m + 1) * 4, :].rearrange("p h d -> p (h d)"), s, free)
                    e_ = cp(act, dst[:, :, slot, :], bank.rearrange("p (m c) -> p m c", m=NQ4), t,
                            slot_free[slot])
                    ring.give(i, e_)
                qk_free[n % 2] = (t,)
                made[n] = (e_, sv)
                yield

            def tile(n):
                bb = n // TB
                first = n % TB == 0
                while n not in made:
                    yield
                ready = made[n]
                lo = P if first else 0
                yield from need((AO, 1), (AOT, 1))
                iao, ao, fao = AO.take()
                s_ao = None
                for g8 in range(2):
                    yield from need((Pm, 4), (ring, 4))
                    groups = []
                    for r in range(4):
                        i, bank, free = ring.take()
                        v = bank.rearrange("p (h n) -> p h n", h=2)
                        mk_ = mm(v, identb, window.unsqueeze(1).broadcast_to([P, 2, 2 * P]), free, m_in, stop=False)
                        groups.append((i, v))
                    for r in range(4):
                        v = groups[r][1]
                        rr = slice(32 * r, 32 * r + AD)
                        for j in range(2):
                            m = 2 * g8 + j
                            for kt in ((1,) if first else (0, 1)):
                                ks = (n - 1 + kt) % 3
                                o_ = v[:, j, kt * P:(kt + 1) * P]
                                t = mm(o_, QT[rr, m, n % 3, :], KT[rr, m, ks, :], ready, mk_,
                                       start=False, stop=True, tp=(32 * r, 0))
                        groups[r] += (t,)
                    pms = []
                    for r, (i, v, t) in enumerate(groups):
                        ip, p_, fp = Pm.take()
                        ms = mx[:, ip, :]
                        s = dve(lambda e, v=v, ms=ms: e.tensor_reduce(ms, v[:, :, lo:], AX, ALU.max, negate=True),
                                t, fp)
                        s = ts(ms, ms, AD ** -0.5, None, ALU.mult)
                        for j in range(2):
                            s = af(p_[:, j, lo:], v[:, j, lo:], ACT.Exp, s, fp,
                                   bias=mx[:, ip, j:j + 1], scale=AD ** -0.5)
                        ring.give(i, s)
                        pms.append((ip, p_, s))
                    yield
                    yield from need((PTm, 4), (ring, 1))
                    pts = []
                    for r, (ip, p_, s) in enumerate(pms):
                        i, bank, free = ring.take()
                        v = bank.rearrange("p (h n) -> p h n", h=2)
                        for j in range(2):
                            for kt in ((1,) if first else (0, 1)):
                                t = tr(v[:, j, kt * P:(kt + 1) * P], p_[:, j, kt * P:(kt + 1) * P], s, free)
                        Pm.give(ip, t)
                        ipt, pt, fpt = PTm.take()
                        s2 = cp(dve if r % 2 else act, pt[:, :, lo:], v[:, :, lo:], t, fpt)
                        ring.give(i, s2)
                        pts.append((ipt, pt, s2))
                    yield
                    yield from need((ring, 2), (OTm, 1))
                    i, bank, free = ring.take()
                    for r, (ipt, pt, s2) in enumerate(pts):
                        for j in range(2):
                            hh = (2 * g8 + j) * 4 + r
                            for kt in ((1,) if first else (0, 1)):
                                t = mm(bank[32 * r:32 * r + 32, j * P:(j + 1) * P], V[:, (n - 1 + kt) % 3, hh, :],
                                       pt[:, j, kt * P:(kt + 1) * P], s2, free,
                                       start=kt == (1 if first else 0), stop=kt == 1, tp=(0, 32 * r))
                        PTm.give(ipt, t)
                    io, ot, fo = OTm.take()
                    s = cp(act, ot, bank[:, 0:2 * P].rearrange("p (j c) -> p j c", j=2), t, fo)
                    ring.give(i, s)
                    last_av = t
                    yield
                    i, bank, free = ring.take()
                    for j in range(2):
                        t = tr(bank[:, j * P:(j + 1) * P], ot[:, j, :], s, free)
                    OTm.give(io, t)
                    v8 = bank[:, 0:8 * 32].rearrange("p (h n) -> p h n", h=8)
                    s = dve(lambda e, v8=v8: e.reciprocal(rec[:, :], v8[:, :, AD]), t)
                    s_ao = tt(ao[:, g8 * 8:(g8 + 1) * 8, :], v8[:, :, 0:AD], bc(rec[:, :], AD), ALU.mult, fao)
                    ring.give(i, s_ao)
                slot_free[(n - 1) % 3] = (last_av,)
                if (n + 1) % TB == 0:
                    slot_free[n % 3] = (last_av,)
                iat, at_, fat = AOT.take()
                i, bank, free = ring.take()
                for k in range(KD):
                    t = tr(bank[:, k * P:(k + 1) * P], ao.rearrange("p h d -> p (h d)")[:, k * P:(k + 1) * P],
                           s_ao, free)
                AO.give(iao, t)
                s2 = cp(act, at_, bank[:, 0:D].rearrange("p (k c) -> p k c", k=KD), t, fat)
                ring.give(i, s2)
                done_tiles.add(n)
                yield
                i, bank, free = ring.take()
                for k in range(KD):
                    t = mm(bank[:, 0:D], at_[:, k, :], W["d_wo"][:, k, :], s2, free, start=k == 0, stop=k == KD - 1)
                AOT.give(iat, t)
                s = tt(X[:, n, :], X[:, n, :], bo[:, :], ALU.add, w_in)
                s = tt(X[:, n, :], X[:, n, :], bank[:, 0:D], ALU.add, t)
                ring.give(i, s)
                state["x"][n] = s

            done_tiles = set()

            def everything():
                for n in range(NT):
                    while n >= 2 and (n - 2) not in done_tiles:
                        yield
                    yield from project(n)
            weave([normed, everything()] + [tile(n) for n in range(NT)], 3)
            state["xt_free"] = (pe.last(),)
            state["fence"] = wait_all()

        def stage_e():
          with ExitStack() as sx:
            t_ = lambda name, shape, dt=F32: sb("e_" + name, shape, dt, ctx=sx)
            W, w_in, _ = state["weights_E"]
            MT = AH * 32 // P
            ctxT = t_("ctx", [P, KD, B * S2])
            bq, bk = t_("bq", [P, MT]), t_("bk", [P, MT])
            bv, bo = t_("bv", [P, D]), t_("bo", [P, D])
            mask8 = t_("mask8", [P, NT, S2], U8)
            keep = t_("keep", [P, NT, S2])
            w_in = c_w["E"].start(sp, ctxT[:, :, :], a["ctxT"].rearrange("(k p) n -> p k n", p=P))
            w_in = c_w["E"].start(sp, bq[:, :], a["e_bq"]); w_in = c_w["E"].start(sp, bk[:, :], a["e_bk"])
            w_in = c_w["E"].start(sp, mask8[:, :, :], a["mask"].rearrange("(n p) s -> p n s", p=P))
            w_in = rows("E", "e_bv", bv[:, :]); w_in = rows("E", "e_bo", bo[:, :])
            ring = Ring([b_[:, :] for b_ in banks])
            s = ts(keep[:, :, :], mask8[:, :, :], -2e38, 1e38, ALU.mult, ALU.add, w_in, lane=pool)
            k_ready = ts(keep[:, :, :], keep[:, :, :], -1e9, None, ALU.max, lane=pool)
            KT = t_("KT", [P, MT, B * S2])
            V = t_("V", [HALF, B, 2, AH, 32])
            pool(lambda e: e.memset(V[:, :, :, :, AD:], 0.0))
            kv_ready = [pool(lambda e: e.memset(V[:, :, :, :, AD:AD + 1], 1.0)), k_ready]
            OTm = Ring([t_(f"OT{i}", [P, 2, P])[:, :, :] for i in range(3)])
            for m in range(MT):
                i, bank, free = ring.take()
                for k in range(KD):
                    t = mm(bank[:, 0:B * S2], W["e_wk"][:, k, m * P:(m + 1) * P], ctxT[:, k, :], free, w_in,
                           start=k == 0, stop=k == KD - 1)
                s = af(KT[:, m, :], bank[:, 0:B * S2], ACT.Identity, t, bias=bk[:, m:m + 1])
                ring.give(i, s)
            kv_ready.append(s)
            xt = []
            normed = layer_norm(ring, xt)
            next(normed)
            for bb in range(B):
                for hf in range(2):
                    i, bank, free = ring.take()
                    lo = bb * S2 + hf * HALF
                    for k in range(KD):
                        t = mm(bank[0:HALF, 0:D], ctxT[:, k, lo:lo + HALF], W["e_wv"][:, k, :],
                               free, start=k == 0, stop=k == KD - 1)
                    s = tt(V[:, bb, hf, :, 0:AD], bank[0:HALF, 0:D].rearrange("p (h d) -> p h d", d=AD),
                           bv[0:HALF, :].rearrange("p (h d) -> p h d", d=AD), ALU.add, t)
                    ring.give(i, s)
            kv_ready.append(s)
            sc = AD ** -0.5
            bs = ts(bq[:, :], bq[:, :], sc, None, ALU.mult, ALU.bypass, w_in)
            QT = Ring([t_(f"Q{i}", [P, MT, 4 * P])[:, :, :] for i in range(2)])
            Pm = Ring([t_(f"P{i}", [P, 2, S2])[:] for i in range(8)])
            PTm = Ring([t_(f"PT{i}", [HALF, 2, 2, P])[:] for i in range(8)])
            mx, rec = t_("mx", [P, 8, 2]), t_("rec", [P, 8])
            AO = Ring([t_(f"AO{i}", [P, AH, AD])[:, :, :] for i in range(3)])
            AOT = Ring([t_(f"AOT{i}", [P, KD, P])[:, :, :] for i in range(3)])
            qs_ = {}

            def queries(n4):
                iq, q, fq = QT.take()
                yield from until(xt, 4 * n4 + 4)
                for m in range(MT):
                    i, bank, free = ring.take()
                    for k in range(KD):
                        t = mm(bank[:, :], W["e_wq"][:, k, m * P:(m + 1) * P],
                               XT[:, k, n4 * 4 * P:(n4 + 1) * 4 * P], free, xt[4 * n4 + 3], w_in,
                               start=k == 0, stop=k == KD - 1)
                    s1 = af(q[:, m, :], bank, ACT.Identity, t, bs, fq, bias=bq[:, m:m + 1], scale=sc)
                    ring.give(i, s1)
                    yield
                qs_[n4] = (iq, q, s1)

            def tile(n):
                while n // 4 not in qs_:
                    yield
                iq, q, qs = qs_[n // 4]
                q = q[:, :, (n % 4) * P:(n % 4 + 1) * P]
                bb = n // TB
                yield from need((AO, 1), (AOT, 1))
                iao, ao, fao = AO.take()
                for g8 in range(2):
                    yield from need((Pm, 4), (ring, 4))
                    groups = []
                    for r in range(4):
                        i, bank, free = ring.take()
                        v = bank[:, 0:2 * S2].rearrange("p (h n) -> p h n", h=2)
                        rr = slice(32 * r, 32 * r + AD)
                        for j in range(2):
                            m = 2 * g8 + j
                            t = mm(v[:, j, :], q[rr, m, :], KT[rr, m, bb * S2:(bb + 1) * S2], free, qs, kv_ready,
                                   tp=(32 * r, 0))
                        ip, p_, fp = Pm.take()
                        s = tt(p_, v, keep[:, n, :].unsqueeze(1).broadcast_to([P, 2, S2]), ALU.min, t, fp)
                        ring.give(i, s)
                        ms = mx[:, ip, :]
                        s = dve(lambda e, p_=p_, ms=ms: e.tensor_reduce(ms, p_, AX, ALU.max, negate=True))
                        for j in range(2):
                            s = af(p_[:, j, :], p_[:, j, :], ACT.Exp, s, bias=mx[:, ip, j:j + 1])
                        groups.append((ip, p_, s))
                    yield
                    yield from need((PTm, 4), (ring, 1))
                    pts = []
                    for r, (ip, p_, s) in enumerate(groups):
                        i, bank, free = ring.take()
                        v = bank[0:HALF, :].rearrange("p (a b c) -> p a b c", a=2, b=2)
                        for j in range(2):
                            for hf in range(2):
                                t = tr(v[:, j, hf, :], p_[:, j, hf * HALF:(hf + 1) * HALF], s, free)
                        Pm.give(ip, t)
                        ipt, pt, fpt = PTm.take()
                        s2 = cp(act if r % 2 else dve, pt, v, t, fpt)
                        ring.give(i, s2)
                        pts.append((ipt, pt, s2))
                    yield
                    yield from need((ring, 2), (OTm, 1))
                    i, bank, free = ring.take()
                    for r, (ipt, pt, s2) in enumerate(pts):
                        for j in range(2):
                            hh = (2 * g8 + j) * 4 + r
                            for hf in range(2):
                                t = mm(bank[32 * r:32 * r + 32, j * P:(j + 1) * P], V[:, bb, hf, hh, :],
                                       pt[:, j, hf, :], s2, free, start=hf == 0, stop=hf == 1, tp=(0, 32 * r))
                        PTm.give(ipt, t)
                    io, ot, fo = OTm.take()
                    s = cp(act, ot, bank[:, 0:2 * P].rearrange("p (j c) -> p j c", j=2), t, fo)
                    ring.give(i, s)
                    yield
                    i, bank, free = ring.take()
                    for j in range(2):
                        t = tr(bank[:, j * P:(j + 1) * P], ot[:, j, :], s, free)
                    OTm.give(io, t)
                    v8 = bank[:, 0:8 * 32].rearrange("p (h n) -> p h n", h=8)
                    s = dve(lambda e, v8=v8: e.reciprocal(rec[:, :], v8[:, :, AD]), t)
                    s_ao = tt(ao[:, g8 * 8:(g8 + 1) * 8, :], v8[:, :, 0:AD], bc(rec[:, :], AD), ALU.mult, fao)
                    ring.give(i, s_ao)
                if n % 4 == 3:
                    QT.give(iq, t)
                iat, at_, fat = AOT.take()
                i, bank, free = ring.take()
                for k in range(KD):
                    t = tr(bank[:, k * P:(k + 1) * P], ao.rearrange("p h d -> p (h d)")[:, k * P:(k + 1) * P],
                           s_ao, free)
                AO.give(iao, t)
                s2 = cp(act, at_, bank[:, 0:D].rearrange("p (k c) -> p k c", k=KD), t, fat)
                ring.give(i, s2)
                yield
                i, bank, free = ring.take()
                for k in range(KD):
                    t = mm(bank[:, 0:D], at_[:, k, :], W["e_wo"][:, k, :], s2, free, start=k == 0, stop=k == KD - 1)
                AOT.give(iat, t)
                s = tt(X[:, n, :], X[:, n, :], bo[:, :], ALU.add, w_in)
                s = tt(X[:, n, :], X[:, n, :], bank[:, 0:D], ALU.add, t)
                ring.give(i, s)
                state["x"][n] = s

            def all_queries():
                for n4 in range(NT // 4):
                    while not QT.free:
                        yield
                    yield from queries(n4)
            weave([normed, all_queries()] + [tile(n) for n in range(NT)], 5)
            state["xt_free"] = (pe.last(),)
            state["fence"] = wait_all()

        def stage_f():
          with ExitStack() as sx:
            t_ = lambda name, shape, dt=F32: sb("f_" + name, shape, dt, ctx=sx)
            xt = []
            NEX = NE1 + NSH
            NR = 5
            wr = [wa[:, i * 3 * D:(i + 1) * 3 * D] for i in range(NR)]
            c_e = [ch(f"expert_in{i}") for i in range(NR)]
            gw, gb = t_("gw", [P, KD, NE1]), t_("gb", [P, NE1])
            c_g = ch("gate_in")
            c_g.start(sp, gw[:, :, :], a["f_gate"].rearrange("(k p) n -> p k n", p=P))
            g_in = c_g.start(sp, gb[:, :], a["f_gb"].rearrange("(o n) -> o n", o=1).broadcast_to([P, NE1]))

            def fetch(j, *after):
                w, c, e_ = wr[j % NR], c_e[j % NR], (NE1 + j) % NEX
                c.start(sp, w[:, 0:2 * D].rearrange("p (k n) -> p k n", k=4), a["f_gu"][e_]
                        .rearrange("(k p) n -> p k n", p=P), *after)
                return c.start(sp, w[:, 2 * D:3 * D], a["f_d"][e_], *after)

            fetched = [fetch(e_, state["wa_free"]) for e_ in range(NR)]
            ring = Ring([b_[:, :] for b_ in banks])
            xt = []
            XH, XL = (t_(name, [P, KD, B * T], F32R) for name in ("XH", "XL"))
            Wp = Ring([t_(f"wp{i}", [P, 2, 3 * D], F32R)[:, :, :] for i in range(2)])
            whole = lambda part: part.bitcast(F32)
            normed = layer_norm(ring, xt, parts=(XH, XL))
            NTE = [P, NT, NE1]
            sc_, ch_, mk, w_ = t_("sc", NTE), t_("ch", NTE), t_("mk", NTE), t_("w", NTE)
            routed = {}

            def route():
                i, bank, free = ring.take()
                for n in range(NT):
                    yield from until(xt, n + 1)
                    for j in range(2 * KD):
                        part = (XH, XL)[j % 2]
                        t = mm(bank[:, n * NE1:(n + 1) * NE1], whole(part[:, j // 2, n * P:(n + 1) * P]), gw[:, j // 2, :],
                               free, xt[n], g_in, start=j == 0, stop=j == 2 * KD - 1)
                s = af(sc_[:], bank.rearrange("p (n e) -> p n e", n=NT), ACT.Exp, t, scale=-1.0)
                ring.give(i, s)
                s = ts(sc_[:], sc_[:], 1.0, None, ALU.add, ALU.bypass, s)
                s = dve(lambda e: e.reciprocal(sc_[:], sc_[:]))
                s = tt(ch_[:], sc_[:], gb[:, :].unsqueeze(1).broadcast_to(NTE), ALU.add, g_in)
                top = t_("top", [P, NT * NG, 8])
                gs = t_("gs", [P, NT, NG])
                G4 = [P, NT, NG, NG]
                c1, c2 = t_("c1", G4), t_("c2", G4)
                for j in range(NT * NG):
                    s = dve(lambda e, j=j: e.max(top[:, j, :], ch_[:].rearrange("p n (g m) -> p (n g) m", g=NG)[:, j, :]))
                    if j % 16 == 15:
                        yield
                s = tt(gs[:].rearrange("p n g -> p (n g)"), top[:, :, 0], top[:, :, 1], ALU.add)
                yield
                me, other = gs[:].unsqueeze(3).broadcast_to(G4), gs[:].unsqueeze(2).broadcast_to(G4)
                f3 = lambda x: x[:].rearrange("p n g m -> p n (g m)")
                s = tt(c1[:], other, me, ALU.is_equal)
                s = tt(f3(c1), f3(c1), const("earlier").unsqueeze(1).broadcast_to([P, NT, NG * NG]), ALU.mult, const_in)
                yield
                s = tt(c2[:], other, me, ALU.is_gt)
                s = tt(c1[:], c1[:], c2[:], ALU.add)
                s = dve(lambda e: e.reduce_sum(gs[:], c1[:], AX))
                s = ts(gs[:], gs[:], float(TOPG), None, ALU.is_lt)
                g8 = gs[:].rearrange("p n g -> p (n g)").unsqueeze(2).broadcast_to([P, NT * NG, NE1 // NG])
                c8 = ch_[:].rearrange("p n (g m) -> p (n g) m", g=NG)
                s = tt(c8, c8, g8, ALU.mult)
                yield
                for n in range(NT):
                    s = dve(lambda e, n=n: e.max(top[:, n, :], ch_[:, n, :]))
                yield
                th = bc(top[:, 0:NT, 7], NE1)
                s = tt(mk[:], ch_[:], th, ALU.is_gt)
                s = dve(lambda e: e.reduce_sum(c1[:, :, 0, 0], mk[:], AX))
                s = ts(c1[:, :, 0, 0], c1[:, :, 0, 0], -1.0, float(TOPK), ALU.mult, ALU.add)
                s = tt(ch_[:], ch_[:], th, ALU.is_equal)
                yield
                for n in range(NT):
                    s = dve(lambda e, n=n: e.tensor_tensor_scan(w_[:, n, :], ones[:, 0:NE1], ch_[:, n, :], 0.0,
                                                                ALU.mult, ALU.add))
                yield
                s = tt(w_[:], w_[:], bc(c1[:, :, 0, 0], NE1), ALU.is_le)
                s = tt(w_[:], w_[:], ch_[:], ALU.mult)
                s = tt(w_[:], w_[:], mk[:], ALU.add)
                yield
                s = tt(w_[:], w_[:], sc_[:], ALU.mult)
                s = dve(lambda e: e.reduce_sum(c1[:, :, 0, 0], w_[:], AX))
                s = ts(c1[:, :, 0, 0], c1[:, :, 0, 0], 1e-20, None, ALU.add)
                s = dve(lambda e: e.reciprocal(c1[:, :, 0, 0], c1[:, :, 0, 0]))
                s = ts(c1[:, :, 0, 0], c1[:, :, 0, 0], RSCALE, None, ALU.mult)
                routed["w"] = tt(w_[:], w_[:], bc(c1[:, :, 0, 0], NE1), ALU.mult)

            Hs = Ring([(t_(f"H{i}", [P, 4 * P])[:, :], t_(f"Hp{i}", [P, 2, 4 * P], F32R)[:, :, :])
                       for i in range(3)])
            Gs = Ring([t_(f"G{i}", [P, 4 * P])[:, :] for i in range(3)])
            order = list(range(NE1, NEX)) + list(range(NE1))
            parts = {}

            def split(j):
                yield from need((Wp, 1))
                iw, wp, fw = Wp.take()
                w = wr[j % NR]
                s = cp(act, wp[:, 0], w, fetched[j], fw)
                s = tt(wp[:, 1], w, whole(wp[:, 0]), ALU.subtract, s, lane=pool)
                parts[j] = (iw, wp, s)
                if j + NR < NEX:
                    fetched.append(fetch(j + NR, s))

            def mm3(out_, lhsT, rhs, k, nk, *after):
                for n, (x, y) in enumerate(((1, 0), (0, 1), (0, 0))):
                    t = mm(out_, lhsT[x], rhs[y], *after, start=n == 0 and k == 0, stop=n == 2 and k == nk - 1)
                return t

            def piece(j, n4):
                e_ = order[j]
                if n4 == 1 and j + 1 < NEX:
                    yield from split(j + 1)
                while j not in parts:
                    yield
                iw, wp, w_in = parts[j]
                tok = slice(n4 * 4 * P, (n4 + 1) * 4 * P)
                yield from until(xt, 4 * n4 + 4)
                yield from need((ring, 2), (Gs, 1), (Hs, 1))
                bks = []
                for lo in (0, D):
                    i, bank, free = ring.take()
                    for k in range(KD):
                        cols = slice(lo + k * FI, lo + (k + 1) * FI)
                        t = mm3(bank, (wp[:, 0, cols], wp[:, 1, cols]), (XH[:, k, tok], XL[:, k, tok]), k, KD,
                                free, w_in, xt[n4 * 4 + 3])
                    bks.append((i, bank, t))
                ig, g_, fg = Gs.take()
                s = af(g_, bks[0][1], ACT.Silu, bks[0][2], fg)
                ring.give(bks[0][0], s)
                ih, (h_, hp), fh = Hs.take()
                s = tt(h_, bks[1][1], g_, ALU.mult, bks[1][2], s, fh)
                ring.give(bks[1][0], s); Gs.give(ig, s)
                s = cp(act, hp[:, 0], h_, s)
                s = tt(hp[:, 1], h_, whole(hp[:, 0]), ALU.subtract, s)
                yield
                yield
                while e_ < NE1 and "w" not in routed:
                    yield
                for half in range(2):
                    yield from need((ring, 1))
                    i, bank, free = ring.take()
                    for m in range(2):
                        cols = slice((2 * half + m) * P, (2 * half + m + 1) * P)
                        t = mm3(bank[:, m * D:(m + 1) * D], (hp[:, 0, cols], hp[:, 1, cols]),
                                (wp[:, 0, 2 * D:3 * D], wp[:, 1, 2 * D:3 * D]), 0, 1, s, free)
                    for m in range(2):
                        n = n4 * 4 + 2 * half + m
                        if e_ < NE1:
                            sx_ = stt(X[:, n, :], bank[:, m * D:(m + 1) * D], w_[:, n, e_:e_ + 1], X[:, n, :],
                                      ALU.mult, ALU.add, t, routed["w"])
                        else:
                            sx_ = tt(X[:, n, :], bank[:, m * D:(m + 1) * D], X[:, n, :], ALU.add, t)
                        state["x"][n] = sx_
                    ring.give(i, sx_)
                Hs.give(ih, t)
                if n4 == 3:
                    Wp.give(iw, t)

            finish(split(0))
            finish(normed)
            weave([route()] + [piece(j, n4) for j in range(NEX) for n4 in range(4)], 4)
            state["xt_free"] = (pe.last(),)
            state["fence"] = wait_all()
        def stage_c():
          with ExitStack() as sx:
            t_ = lambda name, shape, dt=F32: sb("c_" + name, shape, dt, ctx=sx)
            FT, SB = FF // P, CAP // P
            normed = nc.dram_tensor("normed", [B * T, D], F32).ap()
            summed = nc.dram_tensor("summed", [B * T, D], F32).ap()
            c_n, c_s, c_c = [ch("normed_out0"), ch("normed_out1")], ch("x_out"), ch("c_vectors_in")
            c_wt = [ch(f"ffn_weights_in{i}") for i in range(2)]
            wt = [wa[:, i * 4096:(i + 1) * 4096] for i in range(2)]
            wg, b1, b2 = t_("wg", [P, KD, NE0]), t_("b1", [P, NE0 * FT]), t_("b2", [P, NE0, D])
            c_c.start(sp, wg[:, :, :], a["c_wg"].rearrange("(k p) n -> p k n", p=P))
            c_c.start(sp, b1[:, :], a["c_b1"])
            v_in = c_c.start(sp, b2[:, :, :], a["c_b2"].unsqueeze(0).broadcast_to([P, NE0, D]))

            def fetch(e_, *after):
                w, c = wt[e_ % 2], c_wt[e_ % 2]
                c.start(sp, w[:, 0:2048].rearrange("p (k n) -> p k n", k=KD),
                        a["c_w1"][e_].rearrange("(k p) n -> p k n", p=P), *after)
                return c.start(sp, w[:, 2048:4096].rearrange("p (k n) -> p k n", k=FT),
                               a["c_w2"][e_].rearrange("(k p) n -> p k n", p=P), *after)

            fetched = [fetch(0, state["fence"]), fetch(1, state["fence"])]
            for n2 in range(NT // 2):
                x_out = c_s.start(sp, summed[n2 * 2 * P:(n2 + 1) * 2 * P, :].rearrange("(m p) d -> p m d", p=P),
                                  X[:, 2 * n2:2 * n2 + 2, :], state["x"][2 * n2], state["x"][2 * n2 + 1])
            ring = Ring([b_[:, :] for b_ in banks])
            xt = []
            stored = finish(layer_norm(ring, xt, to_dram=(c_n, normed)))

            ET = [P, NE0, NT]
            S, ge, eq, w3 = t_("S", ET), t_("ge", ET), t_("eq", ET), t_("w3", ET)
            th, cand = t_("th", [P, NE0]), t_("cand", [P, NE0])
            cnt, room = t_("cnt", [P, NE0]), t_("room", [P, NE0])
            i, bank, free = ring.take()
            for n in range(NT):
                for k in range(KD):
                    t = mm(bank[:, n * NE0:(n + 1) * NE0], XT[:, k, n * P:(n + 1) * P], wg[:, k, :], free, xt[n], v_in,
                           start=k == 0, stop=k == KD - 1)
            s = af(S[:], bank[:, 0:NT * NE0].rearrange("p (n e) -> p e n", n=NT), ACT.Exp, t, scale=-1.0)
            ring.give(i, s)
            s = ts(S[:], S[:], 1.0, None, ALU.add, ALU.bypass, s)
            s = dve(lambda e: e.reciprocal(S[:], S[:]))
            s = dve(lambda e: e.memset(th[:, :], 0.0))
            NT3 = 2 ** DIGIT - 1
            C3 = [P, NT3, NE0]
            cands, cnts, best = t_("cands", C3), t_("cnts", C3), t_("best", [P, NE0])
            ges = t_("ges", C3 + [NT])
            digits = const("digits").rearrange("p (b v) -> p b v", v=NT3)
            for b in range(30 // DIGIT):
                s = tt(cands[:].bitcast(I32), bc(digits[:, b, :], NE0).bitcast(I32),
                       th[:, :].unsqueeze(1).broadcast_to(C3).bitcast(I32), ALU.bitwise_or, const_in)
                s = tt(ges[:], S[:].unsqueeze(1).broadcast_to(C3 + [NT]), bc(cands[:], NT), ALU.is_ge)
                s = dve(lambda e: e.reduce_sum(cnts[:], ges[:], AX))
                i, bank, free = ring.take()
                v = bank[:, 0:NT3 * NE0].rearrange("p (v e) -> p v e", v=NT3)
                t = mm(v, ones, cnts[:], s, free)
                s = stt(cands[:], v, float(CAP), cands[:], ALU.is_ge, ALU.mult, t)
                ring.give(i, s)
                s = dve(lambda e: e.tensor_reduce(best[:, :], cands[:].rearrange("p v e -> p e v"), AX, ALU.max))
                s = tt(th[:, :], th[:, :], best[:, :], ALU.max)
            s = tt(ge[:], S[:], bc(th[:, :], NT), ALU.is_gt)
            s = dve(lambda e: e.reduce_sum(cnt[:, :], ge[:], AX))
            s2 = tt(eq[:], S[:], bc(th[:, :], NT), ALU.is_equal)
            fe = lambda x: x[:].rearrange("p e n -> p (e n)")
            i, bank, free = ring.take()
            mm(bank[:, 0:NE0], ones, cnt[:, :], s, free)
            mm(bank[:, P:2 * P], const("tri"), fe(eq), s2)
            t = mm(bank[:, 2 * P:3 * P], ones, fe(eq))
            s = ts(room[:, :], bank[:, 0:NE0], -1.0, float(CAP), ALU.mult, ALU.add, t)

            def rank(out_, tri_, tot_, *after):
                s = cp(dve, w3[:], tot_, *after)
                s = dve(lambda e: e.tensor_tensor_scan(fe(out_), ones[:, 0:P], fe(w3), 0.0, ALU.mult, ALU.add))
                s = tt(out_[:], out_[:], w3[:], ALU.subtract)
                s = cp(dve, w3[:], tri_)
                s = cp(dve, cand[:, :], out_[:, :, 0])
                return tt(out_[:], out_[:], w3[:], ALU.add)

            b3 = lambda lo: bank[:, lo:lo + P].rearrange("p (e n) -> p e n", e=NE0)
            rk_ = t_("rk", ET)
            s = rank(rk_, b3(P), b3(2 * P), s)
            ring.give(i, s)
            s = tt(rk_[:], rk_[:], bc(cand[:, :], NT), ALU.subtract)
            s = tt(rk_[:], rk_[:], bc(room[:, :], NT), ALU.is_le)
            s = tt(rk_[:], rk_[:], eq[:], ALU.mult)
            sel = tt(ge[:], ge[:], rk_[:], ALU.add)
            i, bank, free = ring.take()
            mm(bank[:, P:2 * P], const("tri"), fe(ge), sel, free)
            t = mm(bank[:, 2 * P:3 * P], ones, fe(ge))
            s = rank(rk_, b3(P), b3(2 * P), t)
            ring.give(i, s)
            s = tt(rk_[:], rk_[:], bc(cand[:, :], NT), ALU.subtract)
            s = tt(rk_[:], rk_[:], ge[:], ALU.mult)
            slot = ts(rk_[:], rk_[:], -1.0, None, ALU.add)

            iota = t_("iota", [P, CAP])
            io = pool(lambda e: e.iota(iota[:, :], [[1, CAP]], base=0, channel_multiplier=0,
                                       allow_small_or_imprecise_dtypes=True), state["fence"])
            info = t_("info", [P, NE0, NT, 5], BF16)
            ids = small[:, 3 * P:3 * P + 2 * NT].rearrange("p (n c) -> p n c", c=2)
            for c in range(2):
                s = cp(dve, info[:, :, :, c], ids[:, :, c].unsqueeze(1).broadcast_to(ET), const_in)
            s = cp(dve, eq[:], S[:])
            for c in range(3):
                s = cp(dve, info[:, :, :, 2 + c], eq[:])
                if c < 2:
                    s = tt(eq[:], eq[:], info[:, :, :, 2 + c], ALU.subtract)
            info_ready = s

            Oh = Ring([t_(f"oh{i}", [P, NT, CAP], BF16)[:] for i in range(1)])
            Ex = Ring([t_(f"ex{i}", [P, SB, D])[:] for i in range(2)])
            ExT = Ring([t_(f"exT{i}", [P, KD, CAP])[:] for i in range(2)])
            Hh = Ring([t_(f"h{i}", [P, FT, CAP])[:] for i in range(2)])
            Yb = Ring([t_(f"y{i}", [P, SB, D])[:] for i in range(2)])
            idf = t_("idf", [P, NE0, SB])
            idx = t_("idx", [P, NE0, SB], mybir.dt.uint32)
            gv = t_("gv", [P, NE0, SB])
            c_g = [ch(f"gathered{i}") for i in range(2)]
            c_sc = ch("scattered")
            ready, scattered = {}, [x_out]

            def choose(e_):
                yield from need((Oh, 1), (Ex, 1), (ExT, 1))
                io_, oh, fo = Oh.take()
                for n in range(NT):
                    s = ts(oh[:, n, :], iota[:, :], rk_[:, e_, n:n + 1], None, ALU.is_equal, ALU.bypass,
                           slot, io, fo, info_ready)
                    if n % 4 == 3:
                        yield
                yield from need((ring, 1))
                i, bank, free = ring.take()
                for m in range(SB):
                    for n in range(NT):
                        t = mm(bank[:, m * 5:m * 5 + 5], oh[:, n, m * P:(m + 1) * P], info[:, e_, n, :], s, free,
                               start=n == 0, stop=n == NT - 1)
                Oh.give(io_, t)
                v = bank[:, 0:SB * 5].rearrange("p (m c) -> p m c", c=5)
                s = cp(dve, idf[:, e_, :], v[:, :, 1], t)
                s = stt(idf[:, e_, :], v[:, :, 0], float(P), idf[:, e_, :], ALU.mult, ALU.add)
                s1 = cp(dve, idx[:, e_, :], idf[:, e_, :])
                s = dve(lambda e: e.reduce_sum(gv[:, e_, :], v[:, :, 2:5], AX))
                ring.give(i, s)
                ie, ex, fx = Ex.take()
                for m in range(SB):
                    got = c_g[ie].start(pool, None, None, s1, stored, fx, how=lambda e, m=m, ex=ex: e.indirect_dma_start(
                        ex[:, m, :], None, normed, bass.IndirectOffsetOnAxis(idx[:, e_, m:m + 1], 0),
                        bounds_check=B * T - 1))
                yield
                it, ext, ft = ExT.take()
                yield
                yield from need((ring, 1))
                for m in range(0, SB, 2):
                    yield from need((ring, 1))
                    i, bank, free = ring.take()
                    for j in range(2):
                        for k in range(KD):
                            t = tr(bank[:, (k * 2 + j) * P:(k * 2 + j + 1) * P], ex[:, m + j, k * P:(k + 1) * P],
                                   got, free)
                    s = cp(act, ext[:, :, m * P:(m + 2) * P], bank.rearrange("p (k c) -> p k c", k=KD), t, ft)
                    ring.give(i, s)
                Ex.give(ie, t)
                ready[e_] = (it, ext, s)

            def expert(e_):
                while e_ not in ready:
                    yield
                it, ext, es = ready[e_]
                w1 = wt[e_ % 2][:, 0:2048].rearrange("p (k n) -> p k n", k=KD)
                w2 = wt[e_ % 2][:, 2048:4096].rearrange("p (k n) -> p k n", k=FT)
                yield from need((Hh, 1))
                ih, h, fh = Hh.take()
                for f in range(FT):
                    yield from need((ring, 1))
                    i, bank, free = ring.take()
                    for k in range(KD):
                        t = mm(bank, w1[:, k, f * P:(f + 1) * P], ext[:, k, :], es, free, fetched[e_],
                               start=k == 0, stop=k == KD - 1)
                    s = af(h[:, f, :], bank, ACT.Gelu, t, fh, v_in, bias=b1[:, e_ * FT + f:e_ * FT + f + 1])
                    ring.give(i, s)
                    yield
                ExT.give(it, t)
                yield from need((Yb, 1))
                iy, y, fy = Yb.take()
                for m in range(0, SB, 2):
                    yield from need((ring, 1))
                    i, bank, free = ring.take()
                    for j in range(2):
                        for f in range(FT):
                            t = mm(bank[:, j * D:(j + 1) * D], h[:, f, (m + j) * P:(m + j + 1) * P], w2[:, f, :], s, free,
                                   start=f == 0, stop=f == FT - 1)
                    yy = y[:, m:m + 2, :]
                    s2 = tt(yy, bank.rearrange("p (j d) -> p j d", j=2),
                            b2[:, e_, :].unsqueeze(1).broadcast_to([P, 2, D]), ALU.add, t, fy)
                    ring.give(i, s2)
                    s2 = tt(yy, yy, bc(gv[:, e_, m:m + 2], D), ALU.mult)
                    yield
                Hh.give(ih, t)
                if e_ + 2 < NE0:
                    fetched.append(fetch(e_ + 2, t))
                for m in range(SB):
                    out_ = c_sc.start(pool, None, None, s2, scattered[-1],
                                      how=lambda e, m=m, y=y: e.indirect_dma_start(
                        summed, bass.IndirectOffsetOnAxis(idx[:, e_, m:m + 1], 0), y[:, m, :], None,
                        bounds_check=B * T - 1, compute_op=ALU.add))
                scattered.append(out_)
                Yb.give(iy, out_)

            def chooser():
                for e_ in range(NE0):
                    yield from choose(e_)
            weave([chooser()] + [expert(e_) for e_ in range(NE0)], 2)
            c_x2 = ch("x_back")
            for n in range(NT // 2):
                back = c_x2.start(sp, X[:, 2 * n:2 * n + 2, :],
                                  summed[n * 2 * P:(n + 1) * 2 * P, :].rearrange("(m p) d -> p m d", p=P), scattered[-1])
            state["x"] = [back] * NT
            state["xt_free"] = (pe.last(),)
            state["fence"] = state["wa_free"] = wait_all() + [back]

        table = {"A": stage_a, "B": stage_b, "C": stage_c, "D": stage_d, "E": stage_e, "F": stage_f}
        for k in stages:
            fence = state["fence"]
            for lane in (pe, dve, act, pool, sp):
                lane.gate = fence
            if k == "F":
                before_f.close()
            table[k]()

        c_out = ch("out_written")
        for n in range(NT):
            done = c_out.start(sp, out.rearrange("b (t p) d -> p (b t) d", p=P)[:, n, :], X[:, n, :], state["x"][n])

        for lane in lanes:
            for step in lane.steps:
                for w in step.after:
                    if isinstance(w, Step):
                        w.marked = True
        for lane in lanes:
            count = 0
            for step in lane.steps:
                if step.marked:
                    count += 1
                    step.value = count
        block_ = ctx.enter_context(nc.Block())

        def write(lane, e, final=()):
            seen = {}
            for step in lane.steps:
                for w in step.after:
                    if seen.get(id(w.sem), 0) < w.value:
                        e.wait_ge(w.sem, w.value)
                        seen[id(w.sem)] = w.value
                ins = step.emit(e)
                if step.marked:
                    ins.then_inc(lane.sem, 1)
            for w in final:
                e.wait_ge(w.sem, w.value)

        @block_.tensor
        def _(e):
            write(pe, e)

        @block_.vector
        def _(e):
            write(dve, e)

        @block_.scalar
        def _(e):
            write(act, e)

        @block_.gpsimd
        def _(e):
            write(pool, e)

        @block_.sync
        def _(e):
            write(sp, e, (done,))


def lay_out(i):
    f = np.ascontiguousarray
    wide, _, masks, small = constant_arrays()
    o = {"x": i["x"], "wide": wide, "masks": masks, "small": small}
    o["a_wqkv"] = np.concatenate([i["L0_attn_Wq"], i["L0_attn_Wk"], i["L0_attn_Wv"]], 1)
    o["a_wba"] = np.concatenate([i["L0_attn_Wb"], i["L0_attn_Wa"]], 1)
    o["a_wg"], o["a_wo"] = i["L0_attn_Wg"], i["L0_attn_Wo"]
    o["a_conv"] = np.concatenate([i["L0_attn_wq_conv"], i["L0_attn_wk_conv"], i["L0_attn_wv_conv"]], 0)
    o["a_alog"], o["a_dtb"], o["a_onw"] = i["L0_attn_A_log"], i["L0_attn_dt_bias"], i["L0_attn_o_norm_weight"]
    o["ctxT"] = i["ctx_1024"].reshape(B * S2, D).T
    cols = lambda v: v.reshape(-1, P).T
    kv = i["L0_xattn_Wkv"].reshape(XH, 2, XD, D)
    bkv = i["L0_xattn_bkv"].reshape(XH, 2, XD)
    o["b_wq"] = i["L0_xattn_Wq"].T
    o["b_wk"], o["b_wv"] = kv[:, 0].reshape(XH * XD, D).T, kv[:, 1].reshape(XH * XD, D).T
    o["b_wo"] = i["L0_xattn_Wo"].T
    o["b_bq"], o["b_bk"], o["b_bv"] = cols(i["L0_xattn_bq"]), cols(bkv[:, 0]), bkv[:, 1].reshape(-1)
    o["b_bo"] = i["L0_xattn_bo"]
    o["d_wqkv"], o["d_wo"], o["d_bo"] = i["L1_attn_Wqkv"].T, i["L1_attn_Wproj"].T, i["L1_attn_bproj"]

    def spread(w):
        wide_ = np.zeros((AH, 32) + w.shape[1:], w.dtype)
        wide_[:, 0:AD] = w.reshape((AH, AD) + w.shape[1:])
        return wide_.reshape((AH * 32,) + w.shape[1:])

    o["e_wq"], o["e_wk"] = spread(i["L1_xattn_Wq"]).T, spread(i["L1_xattn_Wk"]).T
    o["e_bq"], o["e_bk"] = cols(spread(i["L1_xattn_bq"])), cols(spread(i["L1_xattn_bk"]))
    o["e_wv"], o["e_wo"] = i["L1_xattn_Wv"].T, i["L1_xattn_Wo"].T
    o["e_bv"], o["e_bo"] = i["L1_xattn_bv"], i["L1_xattn_bo"]
    o["mask"] = i["mask_BxSxS2_bk1"].reshape(B * T, S2)
    by_fi = lambda w: w.reshape(NSH, FI, D)
    gate = np.concatenate([i["L1_ffn_expert_gate"], by_fi(i["L1_ffn_shared_gate"])], 0)
    up = np.concatenate([i["L1_ffn_expert_up"], by_fi(i["L1_ffn_shared_up"])], 0)
    o["f_gu"] = np.concatenate([gate.transpose(0, 2, 1), up.transpose(0, 2, 1)], 1)
    sd = i["L1_ffn_shared_down"].T.reshape(NSH, FI, D)
    o["f_d"] = np.concatenate([i["L1_ffn_expert_down"].transpose(0, 2, 1), sd], 0)
    o["f_gate"], o["f_gb"] = i["L1_ffn_gate_w"].T, i["L1_ffn_gate_bias"]
    o["c_wg"] = i["L0_ffn_Wg"]
    o["c_w1"], o["c_w2"] = i["L0_ffn_W1"], i["L0_ffn_W2"]
    o["c_b1"] = i["L0_ffn_b1"].reshape(NE0, FF // P, P).transpose(2, 0, 1).reshape(P, NE0 * FF // P)
    o["c_b2"] = i["L0_ffn_b2"]
    return {k: f(v) for k, v in o.items()}


def kernel(**inputs):
    import concourse.bacc as _bacc
    from concourse.bass_utils import run_bass_kernel_spmd as _run

    arrays = lay_out({k: np.asarray(v) for k, v in inputs.items()})
    nc = _bacc.Bacc("TRN2", target_bir_lowering=False, num_devices=1)
    args = {n: nc.dram_tensor("in_" + n, v.shape, mybir.dt.from_np(v.dtype), kind="ExternalInput").ap()
            for n, v in arrays.items()}
    out = nc.dram_tensor("out_0", (B, T, D), F32, kind="ExternalOutput").ap()
    program(nc, args, out)
    r = _run(nc, [{"in_" + n: v for n, v in arrays.items()}], core_ids=[0])
    return r.results[0]["out_0"]
```
